# Optimizing a Trainium2 kernel written in Bass

```python
import numpy as np
import jax
import jax.numpy as jnp

def _softmax(x, axis=-1):
    return jax.nn.softmax(x, axis=axis)

def _gelu(x):
    return jax.nn.gelu(x, approximate=True)

def _silu(x):
    return jax.nn.silu(x)

def _sigmoid(x):
    return jax.nn.sigmoid(x)

def _layernorm(x, axis=-1, eps=1e-05):
    m = jnp.mean(x, axis=axis, keepdims=True)
    v = jnp.var(x, axis=axis, keepdims=True)
    return (x - m) / jnp.sqrt(v + eps)

def _scatter_add(tgt, idx, src, axis=0):
    return tgt.at[idx].add(src)

def _segment_sum(src, seg, n):
    return jax.ops.segment_sum(src, seg, n)
kernel_name = 'mk_adaln_d1_jaxref_r8_88c12a'

def setup_inputs(seed: int=0):
    np.random.seed(seed)
    _w = jnp.asarray

    def _L0_attn_setup():
        import math
        import jax, jax.numpy as jnp
        import numpy as np
        B, T, D = (2, 256, 256)
        NH, NKV = (32, 8)
        HD = D // NH
        key = jax.random.key(seed)
        kx, kq, kk, kv, ko = jax.random.split(key, 5)
        s = 1.0 / math.sqrt(D)
        return {'x': jax.random.normal(kx, (B, T, D), dtype=jnp.float32), 'wq': jax.random.normal(kq, (D, NH * HD), dtype=jnp.float32) * s, 'wk': jax.random.normal(kk, (D, NKV * HD), dtype=jnp.float32) * s, 'wv': jax.random.normal(kv, (D, NKV * HD), dtype=jnp.float32) * s, 'wo': jax.random.normal(ko, (NH * HD, D), dtype=jnp.float32) * s}
    _L0_attn_in = _L0_attn_setup()

    def _L0_ffn_setup():
        import jax, jax.numpy as jnp
        import numpy as np
        TOP_K = 4
        key = jax.random.key(seed)
        ks = jax.random.split(key, 8)
        B, S, D, E, H, HS = (2, 256, 256, 16, 128, 512)
        scaled = lambda k, shape, fan: jax.random.normal(k, shape, jnp.float32) * fan ** (-0.5)
        return {'x': jax.random.normal(ks[0], (B, S, D), jnp.float32), 'w_router': scaled(ks[1], (D, E), D), 'we1': scaled(ks[2], (E, D, H), D), 'we3': scaled(ks[3], (E, D, H), D), 'we2': scaled(ks[4], (E, H, D), H), 'ws1': scaled(ks[5], (D, HS), D), 'ws3': scaled(ks[6], (D, HS), D), 'ws2': scaled(ks[7], (HS, D), HS)}
    _L0_ffn_in = _L0_ffn_setup()
    _L0_c = _w((lambda *s: np.random.randn(*s).astype(np.float32) * 0.05)(2, 256))
    _L0_wmod = _w((lambda *s: np.random.randn(*s).astype(np.float32) * 0.05)(256, 6 * 256) * 256 ** (-0.5))
    _d = {'L0_attn_x': _L0_attn_in['x'], 'L0_attn_wq': _L0_attn_in['wq'], 'L0_attn_wk': _L0_attn_in['wk'], 'L0_attn_wv': _L0_attn_in['wv'], 'L0_attn_wo': _L0_attn_in['wo'], 'L0_ffn_w_router': _L0_ffn_in['w_router'], 'L0_ffn_we1': _L0_ffn_in['we1'], 'L0_ffn_we3': _L0_ffn_in['we3'], 'L0_ffn_we2': _L0_ffn_in['we2'], 'L0_ffn_ws1': _L0_ffn_in['ws1'], 'L0_ffn_ws3': _L0_ffn_in['ws3'], 'L0_ffn_ws2': _L0_ffn_in['ws2'], 'L0_c': _L0_c, 'L0_wmod': _L0_wmod}
    _x0 = _d['L0_attn_x']
    _d['L0_attn_x'] = jax.random.normal(jax.random.fold_in(jax.random.key(seed), 1), (2, 1024, 256), dtype=_x0.dtype)
    del _x0
    return _d

def reference(L0_attn_x, L0_attn_wq, L0_attn_wk, L0_attn_wv, L0_attn_wo, L0_ffn_w_router, L0_ffn_we1, L0_ffn_we3, L0_ffn_we2, L0_ffn_ws1, L0_ffn_ws3, L0_ffn_ws2, L0_c, L0_wmod):

    def _L0_attn_ref(x, wq, wk, wv, wo):
        import math
        import jax, jax.numpy as jnp
        import numpy as np
        B, T, D = (2, 256, 256)
        NH, NKV = (32, 8)
        HD = D // NH
        bsz, seqlen, _ = x.shape
        q = (x @ wq).reshape(bsz, seqlen, NH, HD).transpose(0, 2, 1, 3)
        k = (x @ wk).reshape(bsz, seqlen, NKV, HD).transpose(0, 2, 1, 3)
        v = (x @ wv).reshape(bsz, seqlen, NKV, HD).transpose(0, 2, 1, 3)
        rep = NH // NKV
        k = jnp.repeat(k, rep, axis=1)
        v = jnp.repeat(v, rep, axis=1)
        att = jnp.einsum('bhqd,bhkd->bhqk', q.astype(jnp.float32), k.astype(jnp.float32)) / math.sqrt(HD)
        mask = jnp.triu(jnp.ones((seqlen, seqlen), dtype=bool), k=1)
        att = jnp.where(mask[None, None, :, :], -jnp.inf, att)
        att = jax.nn.softmax(att, axis=-1)
        y = jnp.einsum('bhqk,bhkd->bhqd', att, v.astype(jnp.float32)).astype(q.dtype)
        y = y.transpose(0, 2, 1, 3).reshape(bsz, seqlen, NH * HD)
        return y @ wo

    def _L0_ffn_ref(x, w_router, we1, we3, we2, ws1, ws3, ws2):
        import jax, jax.numpy as jnp
        import numpy as np
        TOP_K = 4
        B, S, D = x.shape
        T = B * S
        E = w_router.shape[1]
        xt = x.reshape(T, D)
        probs = jax.nn.softmax(xt @ w_router, axis=-1)
        top_w, top_i = jax.lax.top_k(probs, TOP_K)
        top_w = top_w / jnp.sum(top_w, axis=-1, keepdims=True)
        cw = jnp.zeros((T, E), xt.dtype).at[jnp.arange(T)[:, None], top_i].add(top_w)
        g = jax.nn.silu(jnp.einsum('td,edh->teh', xt, we1)) * jnp.einsum('td,edh->teh', xt, we3)
        g = g * cw[:, :, None]
        moe_out = jnp.einsum('teh,ehd->td', g, we2)
        shared = jax.nn.silu(xt @ ws1) * (xt @ ws3) @ ws2
        k = TOP_K
        out = shared / (k + 1) + moe_out * (k / (k + 1))
        return out.reshape(B, S, D)
    x = L0_attn_x
    mod = (_silu(L0_c) @ L0_wmod).reshape(L0_c.shape[0], 6, 1, -1)
    sa, ca, ga, sb, cb, gb = (mod[:, 0], mod[:, 1], mod[:, 2], mod[:, 3], mod[:, 4], mod[:, 5])
    ga = (2 * (ga >= 0) - 1) * jnp.maximum(jnp.abs(ga), 0.25)
    gb = (2 * (gb >= 0) - 1) * jnp.maximum(jnp.abs(gb), 0.25)
    h = _layernorm(x, axis=-1) * (1 + ca) + sa
    x = x + ga * _L0_attn_ref(h, L0_attn_wq, L0_attn_wk, L0_attn_wv, L0_attn_wo)
    h = _layernorm(x, axis=-1) * (1 + cb) + sb
    x = x + gb * _L0_ffn_ref(h, L0_ffn_w_router, L0_ffn_we1, L0_ffn_we3, L0_ffn_we2, L0_ffn_ws1, L0_ffn_ws3, L0_ffn_ws2)
    return x

_drawn_inputs = setup_inputs


def setup_inputs(seed=0):
    import zlib

    import numpy as np

    out = dict(_drawn_inputs(seed))
    spreads = {}
    factors = {}
    for name, (base, spread) in spreads.items():
        noise = np.random.default_rng([zlib.crc32(name.encode()), seed]).standard_normal(out[name].shape)
        drawn = base * np.exp(spread * noise) if base else spread * noise
        out[name] = jnp.asarray(drawn.astype(out[name].dtype))
    for name, factor in factors.items():
        out[name] = (out[name] * factor).astype(out[name].dtype)
    return out
```

```python
from contextlib import ExitStack

import concourse.bass as bass
from concourse import mybir

F32 = mybir.dt.float32
F32R = mybir.dt.float32r
BF16 = mybir.dt.bfloat16
U32 = mybir.dt.uint32
ALU = mybir.AluOpType
ACT = mybir.ActivationFunctionType
AX = mybir.AxisListType

P = 128
B, T, D = 2, 1024, 256
NH, NKV, HD = 32, 8, 8
REP = NH // NKV
DC = D // P
TT = 512
TJ = TT // P
NT = B * T // P
GROUPS = B * NKV
TC = T // P
E, H, HS, TOPK = 16, 128, 512, 4
NE = E + HS // H
NEARLY = 8
NLATE = NE - NEARLY
WCOLS = DC * 2 * H + D
W13 = DC * 2 * H
EPS = 1e-5
SCALE = HD ** -0.5
LEAST = -3.0e38
MASKED = -1.0e30
PROD = 4 * HD
STACK = PROD + 2

STEPS = [(0, c, c * P) for c in range(TC // 2)] + [(1, c, max(0, c - TC // 2) * P) for c in range(TC)]
NSTEP = len(STEPS)


def max_units():
    units = []
    for i in range(TC):
        n, key, part = i + 1, 0, 0
        while n >= 4:
            units += [(i, h, 1, key, 4 * P, part) for h in range(REP)]
            n, key, part = n - 4, key + 4 * P, part + 1
        if n >= 2:
            units += [(i, h, 2, key, 2 * P, part) for h in (0, 2)]
            n, key, part = n - 2, key + 2 * P, part + 1
        if n:
            units += [(i, 0, 4, key, P, part)]
    return units


UNITS = max_units()
NU = len(UNITS)
PARTS = 1 + max(u[5] for u in UNITS)
NB = 3
PER_STEP = NU // NSTEP
AHEAD = 2 * PER_STEP
LAG = 2
assert NU % NB == 0 and NU % NSTEP == 0 and NSTEP % (LAG + 1) == 0 and PER_STEP == 3


class Chain:

    def __init__(self, eng, sem, start):
        self.eng, self.sem, self.count, self.start = eng, sem, 0, start

    def link(self, ins):
        self.count += 1
        ins.then_inc(self.sem, 1)
        self.eng.wait_ge(self.sem, self.start + self.count)


def block_kernel(nc, x_in, wq_in, wk_in, wv_in, wo_in, wr_in, we1_in, we3_in, we2_in,
                 ws1_in, ws3_in, ws2_in, c_in, wmod_in, out):
    q_dram = nc.dram_tensor("q_parts", (2, GROUPS * REP * HD, T), F32, kind="Internal").ap()
    k_dram = nc.dram_tensor("k_parts", (2, GROUPS * HD, T), F32, kind="Internal").ap()
    y_dram = nc.dram_tensor("y_sums", (GROUPS, P, T), F32, kind="Internal").ap()
    r_dram = nc.dram_tensor("row_reciprocals", (B, NH, T), F32, kind="Internal").ap()

    x_view = x_in.rearrange("b (n p) d -> p (b n) d", p=P)
    out_view = out.rearrange("b (n p) d -> p (b n) d", p=P)

    whole = ExitStack()
    with whole:
        def sb(stack, name, shape, dt):
            return stack.enter_context(nc.sbuf_tensor(name, shape, dt))

        def sem(name):
            return whole.enter_context(nc.semaphore(name))

        psum = whole.enter_context(nc.psum_tensor("psum", [P, 8, 512], F32))
        bank = [psum[:, i, :] for i in range(8)]

        x_sb = sb(whole, "x_sb", [P, NT, D], F32)
        w_hi = sb(whole, "w_hi", [P, NEARLY, WCOLS], F32R)
        w_lo = sb(whole, "w_lo", [P, NEARLY, WCOLS], F32R)
        gate = sb(whole, "gate", [P, 2, B, D], F32)
        modc = sb(whole, "modc", [P, B, 2, DC, 2], F32)
        ident = sb(whole, "ident", [P, P], F32)
        ident_b = sb(whole, "ident_b", [P, P], BF16)
        wo_sb = sb(whole, "wo_sb", [P, DC, D], F32)
        wr_sb = sb(whole, "wr_sb", [P, DC, E], F32)
        stats = sb(whole, "stats", [P, TJ, 6], F32)
        mv = sb(whole, "mv", [P, TJ, 2], F32)
        sd = sb(whole, "sd", [P, TJ], F32)
        rstd = sb(whole, "rstd", [P, TJ], F32)

        def settled(eng):
            eng.sem_inc(passed, 1)

        passed = sem("passed")

        def layer_norm(dve, link, sqrt_ready, sqrt_done, count, tile, xn):
            settled(dve)
            for j in range(TJ):
                ins = dve.bn_stats(stats[:, j, :], x_sb[:, tile + j, :])
                if j == TJ - 1:
                    link(ins)
            settled(dve)
            for j in range(TJ):
                ins = dve.bn_aggr(mv[:, j, :], stats[:, j, :])
                if j == TJ - 1:
                    link(ins)
            dve.tensor_scalar(sd[:, :], mv[:, :, 1], EPS, None, ALU.add).then_inc(sqrt_ready, 1)
            dve.wait_ge(sqrt_done, count)
            link(dve.reciprocal(rstd[:, :], sd[:, :]))
            for j in range(TJ):
                ins = dve.tensor_scalar(xn[:, j, :], x_sb[:, tile + j, :], mv[:, j, 0:1],
                                        rstd[:, j:j + 1], ALU.subtract, ALU.mult)
            return ins

        attn = ExitStack()
        qa, qb = [[sb(attn, f"{n}{k}", [P, REP, T], F32R) for k in range(2)] for n in ("qa", "qb")]
        ka, kb = [[sb(attn, f"{n}{k}", [P, T], F32R) for k in range(2)] for n in ("ka", "kb")]
        v_all = sb(attn, "v_all", [P, GROUPS, TC, HD], F32)

        pro = ExitStack()
        wq_sb = sb(pro, "wq_sb", [P, DC, NH * HD], F32)
        wk_sb = sb(pro, "wk_sb", [P, DC, NKV * HD], F32)
        wv_sb = sb(pro, "wv_sb", [P, DC, NKV * HD], F32)
        wmod_sb = sb(pro, "wmod_sb", [P, DC, 6 * D], F32)
        c_sb = sb(pro, "c_sb", [P, DC, B], F32)
        c_rep = sb(pro, "c_rep", [P, DC, B, P], F32)
        g_sign = sb(pro, "g_sign", [P, 2, B, D], F32)
        g_size = sb(pro, "g_size", [P, 2, B, D], F32)
        xn = sb(pro, "xn", [P, TJ, D], F32)
        h_t = sb(pro, "h_t", [P, DC, TT], F32)
        q_parts = sb(pro, "q_parts_sb", [P, 2, DC, TT], F32)
        k_parts = sb(pro, "k_parts_sb", [NKV * HD, 2, TT], F32)

        c_in_s, wmod_s, x_s, wqkv_s = sem("c_loaded"), sem("wmod_loaded"), sem("x_loaded"), sem("wqkv_loaded")
        consts_s, c_silu, c_repd = sem("consts_ready"), sem("c_silu"), sem("c_repeated")
        modc_mm, gate_mm, mod_done = sem("modc_mm"), sem("gate_mm"), sem("mod_done")
        d1 = sem("dve_chain1")
        var1, sqrt1, xn1 = sem("var1_ready"), sem("sqrt1_done"), sem("xn1_ready")
        xt_full, ht_ready = sem("xt_full"), sem("ht_ready")
        q_full, k_full, v_full = sem("q_full"), sem("k_full"), sem("v_full")
        hi_done, lo_done, v_done = sem("qk_high_done"), sem("qk_low_done"), sem("v_done")
        q_out, k_out = sem("q_out"), sem("k_out")
        zeros_s = sem("stacks_zeroed")
        NLINK1 = 3
        MODCOLS = [1, 0, 4, 3]

        with nc.Block() as block:
            @block.sync
            def _(sp):
                sp.dma_start(c_sb[:, :, 0], c_in[0, :].rearrange("(c p) -> p c", p=P),
                             allow_slow_non_contiguous=True).then_inc(c_in_s, 16)
                sp.dma_start(c_sb[:, :, 1], c_in[1, :].rearrange("(c p) -> p c", p=P),
                             allow_slow_non_contiguous=True).then_inc(c_in_s, 16)
                for q in range(4):
                    sp.dma_start(x_sb[:, q * TJ:(q + 1) * TJ, :], x_view[:, q * TJ:(q + 1) * TJ, :]).then_inc(x_s, 16)
                sp.dma_start(wq_sb[:], wq_in.rearrange("(c p) n -> p c n", p=P)).then_inc(wqkv_s, 16)
                sp.dma_start(wk_sb[:], wk_in.rearrange("(c p) n -> p c n", p=P)).then_inc(wqkv_s, 16)
                sp.dma_start(wv_sb[:], wv_in.rearrange("(c p) n -> p c n", p=P)).then_inc(wqkv_s, 16)
                sp.dma_start(wo_sb[:], wo_in.rearrange("(c p) n -> p c n", p=P)).then_inc(wqkv_s, 16)
                sp.dma_start(wr_sb[:], wr_in.rearrange("(c p) n -> p c n", p=P)).then_inc(wqkv_s, 16)
                sp.sem_inc(q_out, 16)
                sp.sem_inc(k_out, 16)
                with sp.Fori(0, B) as b:
                    for half in range(2):
                        n = 2 * b + half + 1
                        toks = slice(half * TT, (half + 1) * TT)
                        sp.wait_ge(lo_done, 3 * n + 1)
                        for m in range(DC):
                            for part in range(2):
                                sp.dma_start(q_dram[part, bass.ds(b * NH * HD + m * P, P), toks],
                                             q_parts[:, part, m, :]).then_inc(q_out, 16)
                        for part in range(2):
                            sp.dma_start(k_dram[part, bass.ds(b * NKV * HD, NKV * HD), toks],
                                         k_parts[:, part, :]).then_inc(k_out, 16)
                sp.wait_ge(q_out, 16 + 16 * 16)
                sp.wait_ge(k_out, 16 + 16 * 8)

            @block.gpsimd
            def _(pool):
                pool.dma_start(wmod_sb[:], wmod_in.rearrange("(c p) n -> p c n", p=P)).then_inc(wmod_s, 16)
                pool.memset(ident[:], 0.0).then_inc(consts_s, 1)
                pool.memset(ident_b[:], 0.0).then_inc(consts_s, 1)
                for tile in ka + kb + qa + qb:
                    pool.memset(tile[:].bitcast(F32), 0.0).then_inc(zeros_s, 1)
                pool.wait_ge(consts_s, 2)
                for m in (ident, ident_b):
                    pool.affine_select(out=m[:, :], in_=m[:, :], compare_op=ALU.not_equal, fill=1.0, base=0,
                                       pattern=[[-1, P]], channel_multiplier=1).then_inc(consts_s, 1)

            @block.scalar
            def _(act):
                act.wait_ge(c_in_s, 32)
                act.activation(c_sb[:], c_sb[:], ACT.Silu).then_inc(c_silu, 1)
                with act.Fori(0, B) as b:
                    for half in range(2):
                        n = 2 * b + half + 1
                        act.wait_ge(var1, n)
                        act.activation(sd[:], sd[:], ACT.Sqrt).then_inc(sqrt1, 1)
                        for m in range(DC):
                            act.wait_ge(q_full, 2 * (n - 1) + m + 1)
                            if m == 0:
                                act.wait_ge(q_out, 64 * (n - 1) + 16)
                            act.activation(q_parts[:, 0, m, :].bitcast(F32R), bank[2 + m][:], ACT.Copy)\
                               .then_inc(hi_done, 1)
                        act.wait_ge(k_full, n)
                        act.wait_ge(k_out, 32 * (n - 1) + 16)
                        act.activation(k_parts[:, 0, :].bitcast(F32R), bank[4][0:NKV * HD, :], ACT.Copy)\
                           .then_inc(hi_done, 1)

            @block.tensor
            def _(pe):
                pe.wait_ge(c_silu, 1)
                pe.wait_ge(wmod_s, 16)
                for k, which in enumerate(MODCOLS):
                    for c in range(DC):
                        for kc in range(DC):
                            last = pe.matmul(bank[0][:, (k * DC + c) * B:(k * DC + c + 1) * B],
                                             wmod_sb[:, kc, which * D + c * P:which * D + (c + 1) * P],
                                             c_sb[:, kc, :], start=(kc == 0), stop=(kc == DC - 1))
                last.then_inc(modc_mm, 1)
                pe.wait_ge(c_repd, 1)
                for g, which in enumerate((2, 5)):
                    for b in range(B):
                        for kc in range(DC):
                            last = pe.matmul(bank[6 + g][:, b * D:(b + 1) * D], c_rep[:, kc, b, :],
                                             wmod_sb[:, kc, which * D:(which + 1) * D],
                                             start=(kc == 0), stop=(kc == DC - 1))
                last.then_inc(gate_mm, 1)
                pe.wait_ge(wqkv_s, 16 * 5)
                pe.wait_ge(consts_s, 4)
                pe.wait_ge(mod_done, 1)
                with pe.Fori(0, B) as b:
                    for half in range(2):
                        n = 2 * b + half + 1
                        pe.wait_ge(xn1, n)
                        for c in range(DC):
                            for j in range(TJ):
                                last = pe.transpose(bank[c][:, j * P:(j + 1) * P], xn[:, j, c * P:(c + 1) * P],
                                                    ident[:])
                            last.then_inc(xt_full, 1)
                        pe.wait_ge(ht_ready, 2 * n)
                        pe.wait_ge(lo_done, 3 * (n - 1) + 1)
                        for m in range(DC):
                            for kc in range(DC):
                                last = pe.matmul(bank[2 + m][:], wq_sb[:, kc, m * P:(m + 1) * P], h_t[:, kc, :],
                                                 start=(kc == 0), stop=(kc == DC - 1))
                            last.then_inc(q_full, 1)
                        for kc in range(DC):
                            last = pe.matmul(bank[4][0:NKV * HD, :], wk_sb[:, kc, :], h_t[:, kc, :],
                                             start=(kc == 0), stop=(kc == DC - 1))
                        last.then_inc(k_full, 1)
                        pe.wait_ge(v_done, n)
                        for j in range(TJ):
                            for kc in range(DC):
                                last = pe.matmul(bank[5][:, j * NKV * HD:(j + 1) * NKV * HD],
                                                 h_t[:, kc, j * P:(j + 1) * P], wv_sb[:, kc, :],
                                                 start=(kc == 0), stop=(kc == DC - 1))
                        last.then_inc(v_full, 1)

            @block.vector
            def _(dve):
                dve.sem_inc(v_done, 1)
                dve.sem_inc(lo_done, 1)
                dve.wait_ge(c_silu, 1)
                dve.tensor_copy(c_rep[:], c_sb[:].unsqueeze(3).to_broadcast([P, DC, B, P])).then_inc(c_repd, 1)
                setup = Chain(dve, d1, 0)
                dve.wait_ge(modc_mm, 1)
                for norm in range(2):
                    cols = bank[0][:, 8 * norm:8 * norm + 8].rearrange("p (k c b) -> p b c k", k=2, c=DC)
                    ins = dve.tensor_copy(modc[:, :, norm, :, :], cols)
                setup.link(ins)
                dve.tensor_scalar(modc[:, :, :, :, 0], modc[:, :, :, :, 0], 1.0, None, ALU.add).then_inc(mod_done, 1)
                dve.wait_ge(gate_mm, 1)
                rows = psum[:, 6:8, :].rearrange("p g (b d) -> p g b d", b=B)
                dve.tensor_scalar(g_sign[:], rows, 0.0, 2.0, ALU.is_ge, ALU.mult)
                setup.link(dve.tensor_scalar(g_size[:], rows, -1.0, 0.25, ALU.mult, ALU.max))
                setup.link(dve.tensor_tensor(out=g_size[:], in0=g_size[:], in1=rows, op=ALU.max))
                for g in range(2):
                    ins = dve.scalar_tensor_tensor(out=gate[:, g, :, :], in0=g_sign[:, g, :, :], scalar=-1.0,
                                                   in1=g_size[:, g, :, :], op0=ALU.add, op1=ALU.mult)
                setup.link(ins)
                setup.link(dve.tensor_scalar(gate[:, 1, :, :], gate[:, 1, :, :], 1.0 / (TOPK + 1), None, ALU.mult))
                dve.wait_ge(mod_done, 1)
                dve.wait_ge(x_s, 64)
                with dve.Fori(0, B) as b:
                    for half in range(2):
                        n = 2 * b + half + 1
                        chain = Chain(dve, d1, NLINK1 * (n - 1) + setup.count)
                        layer_norm(dve, chain.link, var1, sqrt1, n, b * TC + half * TJ, xn).then_inc(xn1, 1)
                        assert chain.count == NLINK1
                        for c in range(DC):
                            dve.wait_ge(xt_full, 2 * (n - 1) + c + 1)
                            dve.tensor_scalar(h_t[:, c, :], bank[c][:], modc[:, b, 0, c, 0:1],
                                              modc[:, b, 0, c, 1:2], ALU.mult, ALU.add).then_inc(ht_ready, 1)
                        for m in range(DC):
                            dve.wait_ge(hi_done, 3 * (n - 1) + m + 1)
                            dve.tensor_tensor(out=q_parts[:, 1, m, :].bitcast(F32R), in0=bank[2 + m][:],
                                              in1=q_parts[:, 0, m, :], op=ALU.subtract).then_inc(lo_done, 1)
                        dve.wait_ge(hi_done, 3 * n)
                        dve.tensor_tensor(out=k_parts[:, 1, :].bitcast(F32R), in0=bank[4][0:NKV * HD, :],
                                          in1=k_parts[:, 0, :], op=ALU.subtract).then_inc(lo_done, 1)
                        dve.wait_ge(v_full, n)
                        dve.tensor_copy(v_all[:, bass.ds(b * NKV, NKV), half * TJ:(half + 1) * TJ, :]
                                        .rearrange("p g j d -> p j g d"),
                                        bank[5][:, 0:TJ * NKV * HD].rearrange("p (j g d) -> p j g d", j=TJ, g=NKV))\
                           .then_inc(v_done, 1)
        pro.close()

        core = ExitStack()
        probs = sb(core, "probs", [P, LAG + 1, REP, TT], F32)
        v_aug = sb(core, "v_aug", [P, 2, TC, 32], F32)
        y_sb = sb(core, "y_sb", [P, 2, TT], F32)
        max_parts = sb(core, "max_parts", [P, REP, TC, PARTS], F32)
        neg_max = sb(core, "neg_max", [P, 2, REP * TC], F32)
        neg_max_f = sb(core, "neg_max_f", [P, REP * TC], F32)
        neg_max_t = sb(core, "neg_max_t", [2 * REP * TC, P], F32)
        w_raw = sb(core, "w_raw", [P, 2, WCOLS], F32)
        causal = sb(core, "causal", [P, P], BF16)
        ident4 = sb(core, "ident4", [P, REP, P], BF16)

        unit_bank, sum_bank = (4, 5, 6), 7
        qa_in, qb_in, raw_in = [[sem(f"{n}_{k}") for k in range(2)] for n in ("qa_loaded", "qb_loaded", "raw_loaded")]
        row_in, y_out = [[sem(f"{n}_{k}") for k in range(2)] for n in ("max_rows_loaded", "sums_out")]
        consts2, v_aug_s, parts_set = sem("consts2_ready"), sem("v_aug_ready"), sem("max_parts_set")
        unit_full, unit_free = sem("unit_full"), sem("unit_free")
        negm_done, negt_full, negt_done = sem("neg_max_done"), sem("neg_max_t_full"), sem("neg_max_t_done")
        st_full, p_full, p_masked, pv_done = sem("scores_full"), sem("probs_full"), sem("probs_masked"), sem("pv_done")
        y_done, hi2, lo2, d2 = sem("sums_copied"), sem("w_high_done"), sem("w_low_done"), sem("dve_chain2")
        LOADS = 16 * 8
        NDIAG = TC

        def wait_if(eng, s, value):
            if not isinstance(value, int) or value > 0:
                eng.wait_ge(s, value)

        def load_stacks(sp, group, q_tile, k_tile, par, loaded):
            for block8 in range(4):
                row = HD * block8
                q_rows = q_dram[block8 % 2, bass.ds(group * REP * HD, REP * HD), :]
                sp.dma_start(q_tile[par][row:row + HD].bitcast(F32), q_rows.rearrange("(h d) t -> d h t", h=REP))\
                  .then_inc(loaded[par], 16)
                sp.dma_start(k_tile[par][row:row + HD, :].bitcast(F32), k_dram[block8 // 2, bass.ds(group * HD, HD), :])\
                  .then_inc(loaded[par], 16)

        def load_expert(eng, raw, w1, w3, w2, loaded):
            cols = raw[:, 0:W13].rearrange("p (c w h) -> p c w h", c=DC, w=2)
            eng.dma_start(cols[:, :, 0, :], w1.rearrange("(c p) h -> p c h", p=P)).then_inc(loaded, 16)
            eng.dma_start(cols[:, :, 1, :], w3.rearrange("(c p) h -> p c h", p=P)).then_inc(loaded, 16)
            eng.dma_start(raw[:, W13:WCOLS], w2).then_inc(loaded, 16)

        def periods(eng, period):
            period(0, 0)
            period(0, 1)
            with eng.Fori(1, NEARLY // 2) as it:
                period(it, 0)
                period(it, 1)
            with eng.Fori(NEARLY // 2, GROUPS // 2 - 1) as it:
                period(it, 0, weights=False)
                period(it, 1, weights=False)
            period(GROUPS // 2 - 1, 0, last=1)
            period(GROUPS // 2 - 1, 1, last=2)

        def ahead(it, par, s, last):
            for u in range(PER_STEP * s + AHEAD, PER_STEP * (s + 1) + AHEAD):
                if u < NU and last < 2:
                    yield (it + par, 1 - par, u)
                elif u >= NU and last < 1:
                    yield (it + 1, par, u - NU)

        with nc.Block() as block:
            @block.sync
            def _(sp):
                def rows_in(it, par):
                    sp.wait_ge(negt_done, 2 * it + par + 1)
                    for part in range(2):
                        row = PROD + part
                        sp.dma_start(qb[par][row:row + 1].bitcast(F32),
                                     neg_max_t[part * REP * TC:(part + 1) * REP * TC, :]).then_inc(row_in[par], 16)

                def sums_out(group, half):
                    sp.wait_ge(y_done, 2 * group + half + 1)
                    sp.dma_start(y_dram[group, :, half * TT:(half + 1) * TT], y_sb[:, half, :]).then_inc(y_out[half], 16)

                def period(it, par, last=0, weights=True):
                    group = 2 * it + par
                    if last < 2:
                        wait_if(sp, st_full, 2 * NSTEP * group)
                        load_stacks(sp, group + 1, qb, kb, 1 - par, qb_in)
                    if last < 1:
                        sp.wait_ge(unit_full, NU * (group + 1))
                        load_stacks(sp, group + 2, qa, ka, par, qa_in)
                    if weights and last < 1:
                        wait_if(sp, lo2, group - 1)
                        load_expert(sp, w_raw[:, par, :], we1_in[group], we3_in[group], we2_in[group], raw_in[par])
                    if not (isinstance(group, int) and group == 0):
                        sums_out(group - 1, 1)
                    sums_out(group, 0)
                    if last < 2:
                        rows_in(it + par, 1 - par)

                load_stacks(sp, 0, qa, ka, 0, qa_in)
                load_stacks(sp, 0, qb, kb, 0, qb_in)
                load_stacks(sp, 1, qa, ka, 1, qa_in)
                rows_in(0, 0)
                periods(sp, period)
                sums_out(GROUPS - 1, 1)
                for k in range(2):
                    sp.wait_ge(y_out[k], 16 * GROUPS)

            @block.gpsimd
            def _(pool):
                pool.memset(causal[:], 0.0).then_inc(consts2, 1)
                pool.memset(ident4[:], 0.0).then_inc(consts2, 1)
                pool.memset(v_aug[:], 1.0).then_inc(consts2, 1)
                pool.wait_ge(consts2, 3)
                pool.affine_select(out=causal[:, :], in_=causal[:, :], compare_op=ALU.is_ge, fill=MASKED, base=0,
                                   pattern=[[1, P]], channel_multiplier=-1).then_inc(consts2, 1)
                pool.affine_select(out=ident4[:], in_=ident4[:], compare_op=ALU.not_equal, fill=1.0, base=0,
                                   pattern=[[0, REP], [-1, P]], channel_multiplier=1).then_inc(consts2, 1)

                def values(group, par):
                    pool.tensor_copy(v_aug[:, par, :, 0:HD], v_all[:, group, :, :]).then_inc(v_aug_s, 1)

                def period(it, par, last=0, weights=True):
                    group = 2 * it + par
                    for s, (half, c, off) in enumerate(STEPS):
                        if c >= half * (TC // 2):
                            pool.wait_ge(p_full, 2 * NSTEP * group + 2 * s + 2)
                            tile = probs[:, s % (LAG + 1), :, off:off + P]
                            settled(pool)
                            pool.affine_select(out=tile, in_=tile, compare_op=ALU.is_ge, fill=0.0, base=0,
                                               pattern=[[0, REP], [1, P]], channel_multiplier=-1).then_inc(p_masked, 1)
                        if s == 3 and last < 2:
                            wait_if(pool, pv_done, NSTEP * group)
                            values(group + 1, 1 - par)
                        if s == 4 and weights and last < 1:
                            pool.wait_ge(hi2, group + 1)
                            pool.tensor_tensor(out=w_lo[:, group, :], in0=w_raw[:, par, :],
                                               in1=w_hi[:, group, :].bitcast(F32), op=ALU.subtract).then_inc(lo2, 1)

                values(0, 0)
                periods(pool, period)

            @block.scalar
            def _(act):
                def turned(it, par):
                    group = 2 * it + par
                    act.wait_ge(negt_full, group + 1)
                    wait_if(act, row_in[1 - par], 32 * (it + par))
                    act.activation(neg_max_t[:], bank[unit_bank[0]][0:2 * REP * TC, 0:P], ACT.Copy).then_inc(negt_done, 1)

                def sums(group, half):
                    act.wait_ge(pv_done, NSTEP * group + (TC // 2, NSTEP)[half])
                    wait_if(act, y_out[half], 16 * group)
                    act.activation(y_sb[:, half, :], bank[sum_bank][:, :], ACT.Copy).then_inc(y_done, 1)

                def period(it, par, last=0, weights=True):
                    group = 2 * it + par
                    for s, (half, c, off) in enumerate(STEPS):
                        wait_if(act, pv_done, NSTEP * group + s - LAG)
                        for pair in range(2):
                            act.wait_ge(st_full, 2 * NSTEP * group + 2 * s + pair + 1)
                            act.activation(probs[:, s % (LAG + 1), 2 * pair:2 * pair + 2, off:TT],
                                           psum[:, 2 * pair:2 * pair + 2, off:TT], ACT.Exp, scale=SCALE).then_inc(p_full, 1)
                        if s == 1 and not (isinstance(group, int) and group == 0):
                            sums(group - 1, 1)
                        if s == TC // 2 + LAG - 1:
                            sums(group, 0)
                        if s == 3 and weights and last < 1:
                            act.wait_ge(raw_in[par], 48 * (it + 1))
                            act.activation(w_hi[:, group, :], w_raw[:, par, :], ACT.Copy).then_inc(hi2, 1)
                        if s == NSTEP - 2 and last < 2:
                            turned(it + par, 1 - par)

                turned(0, 0)
                periods(act, period)
                sums(GROUPS - 1, 1)

            @block.tensor
            def _(pe):
                def unit(it, par, u):
                    i, h0, nh, key, w, _ = UNITS[u]
                    group, bk = 2 * it + par, bank[unit_bank[u % NB]]
                    if u == 0:
                        pe.wait_ge(qa_in[par], LOADS * (it + 1))
                    wait_if(pe, unit_free, NU * group + u - NB + 1)
                    if u == NB:
                        wait_if(pe, negt_done, group)
                    diag = key + w == (i + 1) * P
                    for k in range(nh):
                        last = pe.matmul(bk[:, k * w:(k + 1) * w], qa[par][:, h0 + k, i * P:(i + 1) * P],
                                         ka[par][:, key:key + w], start=(k == 0),
                                         stop=(k == nh - 1 and not diag), skip_group_check=True)
                    if diag:
                        last = pe.matmul(bk[:, 0:nh * w].rearrange("p (k w) -> p k w", k=nh)[:, :, w - P:w],
                                         causal[:], ident4[:, 0:nh, :], start=False, stop=True, skip_group_check=True)
                    last.then_inc(unit_full, 1)

                def turn(it, par, followed):
                    group = 2 * it + par
                    pe.wait_ge(negm_done, group + 1)
                    pe.wait_ge(unit_free, NU * (group + 1) + followed)
                    settled(pe)
                    pe.transpose(bank[unit_bank[0]][0:2 * REP * TC, 0:P],
                                 neg_max[:].rearrange("p a n -> p (a n)"), ident[:]).then_inc(negt_full, 1)

                def scores(it, par, s, pair):
                    half, c, off = STEPS[s]
                    group = 2 * it + par
                    if s == 0 and pair == 0:
                        pe.wait_ge(qb_in[par], LOADS * (it + 1))
                        pe.wait_ge(row_in[par], 32 * (it + 1))
                    wait_if(pe, p_full, 2 * NSTEP * group + 2 * s + pair - 1)
                    for h in (2 * pair, 2 * pair + 1):
                        last = pe.matmul(bank[h][:, off:TT], kb[par][:, c * P:(c + 1) * P],
                                         qb[par][:, h, half * TT + off:(half + 1) * TT],
                                         start=True, stop=True)
                    last.then_inc(st_full, 1)

                def product(it, par, s):
                    half, c, off = STEPS[s]
                    group = 2 * it + par
                    if s == 0:
                        pe.wait_ge(v_aug_s, group + 1)
                    if c == 0:
                        wait_if(pe, y_done, 2 * group + half)
                    pe.wait_ge(p_full, 2 * NSTEP * group + 2 * s + 2)
                    if c >= half * (TC // 2):
                        pe.wait_ge(p_masked, NDIAG * group + c + 1)
                    for h in range(REP):
                        last = pe.matmul(bank[sum_bank][32 * h:32 * h + 32, off:TT], v_aug[:, par, c, :],
                                         probs[:, s % (LAG + 1), h, off:TT], start=(c == 0),
                                         stop=(c == (TC // 2, TC)[half] - 1), skip_group_check=True)
                    last.then_inc(pv_done, 1)

                def period(it, par, last=0, weights=True):
                    for s in range(NSTEP):
                        units = list(ahead(it, par, s, last))
                        if s == NSTEP - 1 and last < 2:
                            turn(it + par, 1 - par, followed=1 if last == 0 else 0)
                        for k in range(PER_STEP):
                            if k < 2:
                                scores(it, par, s, k)
                            elif s >= LAG:
                                product(it, par, s - LAG)
                            elif par == 1:
                                product(it, 0, s - LAG + NSTEP)
                            elif not isinstance(it, int) or it > 0:
                                product(it - 1, 1, s - LAG + NSTEP)
                            if k < len(units):
                                unit(*units[k])

                pe.wait_ge(consts2, 5)
                pe.wait_ge(parts_set, 3)
                for u in range(NU):
                    unit(0, 0, u)
                for u in range(AHEAD):
                    if u == NB:
                        turn(0, 0, followed=1)
                    unit(0, 1, u)
                periods(pe, period)
                for s in range(NSTEP - LAG, NSTEP):
                    product(GROUPS // 2 - 1, 1, s)

            @block.vector
            def _(dve):
                def unit(it, par, u):
                    i, h0, nh, key, w, part = UNITS[u]
                    group = 2 * it + par
                    dve.wait_ge(unit_full, NU * group + u + 1)
                    dve.tensor_reduce(out=max_parts[:, h0:h0 + nh, i, part],
                                      in_=bank[unit_bank[u % NB]][:, 0:nh * w].rearrange("p (k w) -> p k w", k=nh),
                                      axis=AX.X, op=ALU.max).then_inc(unit_free, 1)
                    if u == NU - 1:
                        dve.wait_ge(unit_free, NU * (group + 1))
                        wait_if(dve, negm_done, group)
                        chain = Chain(dve, d2, 2 * group)
                        chain.link(dve.tensor_reduce(out=neg_max_f[:], in_=max_parts[:].rearrange("p h i a -> p (h i) a"),
                                                     axis=AX.X, op=ALU.max, negate=True))
                        wait_if(dve, negt_full, group)
                        chain.link(dve.tensor_copy(neg_max[:, 0, :].bitcast(F32R), neg_max_f[:]))
                        dve.tensor_tensor(out=neg_max[:, 1, :].bitcast(F32R), in0=neg_max_f[:], in1=neg_max[:, 0, :],
                                          op=ALU.subtract).then_inc(negm_done, 1)

                def period(it, par, last=0, weights=True):
                    for s in range(NSTEP):
                        for at in ahead(it, par, s, last):
                            unit(*at)

                dve.memset(max_parts[:], LEAST).then_inc(parts_set, 1)
                for par in range(2):
                    dve.memset(kb[par][PROD:STACK, :].bitcast(F32), 1.0).then_inc(parts_set, 1)
                dve.wait_ge(parts_set, 3)
                for u in range(NU):
                    unit(0, 0, u)
                for u in range(AHEAD):
                    unit(0, 1, u)
                periods(dve, period)
        core.close()
        attn.close()

        moe = ExitStack()
        h2_hi = sb(moe, "h2_hi", [P, DC, B * T], F32R)
        h2_lo = sb(moe, "h2_lo", [P, DC, B * T], F32R)
        CWR = 3 * E
        cw_t = sb(moe, "cw_t", [CWR, B * T], BF16)
        sel = sb(moe, "sel", [CWR, E, P], BF16)

        post = ExitStack()
        l_sb = sb(post, "l_sb", [P, B, T // 4], F32)
        r_sb = sb(post, "r_sb", [P, B, T // 4], F32)
        y_t = sb(post, "y_t", [P, DC, TT], F32)
        r_t = sb(post, "r_t", [P, DC, TT], F32)
        yn = sb(post, "yn", [P, DC, TT], F32)
        att = sb(post, "att", [P, TJ, D], F32)
        xn2 = sb(post, "xn2", [P, TJ, D], F32)
        h2 = sb(post, "h2", [P, DC, TT], F32)
        iota16 = sb(post, "iota16", [P, E], F32)
        lg = sb(post, "lg", [P, TJ, E], F32)
        lmax = sb(post, "lmax", [P, TJ], F32)
        top = sb(post, "top", [P, TJ, 8], F32)
        top_i = sb(post, "top_i", [P, TJ, 8], U32)
        top_f = sb(post, "top_f", [P, TJ, 8], F32)
        hit = sb(post, "hit", [P, TJ, TOPK, E], F32)
        cw = sb(post, "cw", [P, TJ, E], F32)
        cw_rest = sb(post, "cw_rest", [P, TJ, E], F32)
        wsum = sb(post, "wsum", [P, TJ], F32)
        cw_parts = sb(post, "cw_parts", [P, TJ, 3, E], BF16)

        l_in, l_recip, r_out, y_in, yn_done = sem("l_loaded"), sem("l_reciprocal"), sem("r_out"), sem("y_loaded"), sem("yn_done")
        att_full, att_read, var2, sqrt2, xn2_done = sem("att_full"), sem("att_read"), sem("var2_ready"), sem("sqrt2_done"), sem("xn2_done")
        xt2_full, h2_done, h2_hi_s, h2_lo_s = sem("xt2_full"), sem("h2_done"), sem("h2_high_done"), sem("h2_low_done")
        lg_full, lg_ready, lg_exp, cwp_done = sem("logits_full"), sem("logits_ready"), sem("logits_exp"), sem("cw_parts_done")
        cwt_full, cwt_done, consts3, d3 = sem("cw_t_full"), sem("cw_t_done"), sem("consts3_ready"), sem("dve_chain3")
        NLINK3 = 19
        with nc.Block() as block:
            @block.sync
            def _(sp):
                for b in range(B):
                    rows = y_dram[b * NKV:(b + 1) * NKV].rearrange("g (h r) (q t) -> g h r q t", r=32, q=4)
                    sp.dma_start(l_sb[:, b, :], rows[:, :, HD, :, :]).then_inc(l_in, 16)
                sp.wait_ge(l_recip, 1)
                for b in range(B):
                    sp.dma_start(r_dram[b].rearrange("n (q t) -> (n q) t", q=4), r_sb[:, b, :]).then_inc(r_out, 16)
                sp.wait_ge(r_out, 32)
                with sp.Fori(0, B) as b:
                    for half in range(2):
                        n = 2 * b + half + 1
                        toks = slice(half * TT, (half + 1) * TT)
                        sp.wait_ge(yn_done, n)
                        for m in range(DC):
                            src = y_dram[bass.ds(b * NKV + 4 * m, 4), :, toks].rearrange("g (h r) t -> g h r t", r=32)
                            sp.dma_start(y_t[:, m, :], src[:, :, 0:HD, :]).then_inc(y_in, 16)
                            src = r_dram[b, 16 * m:16 * m + 16, toks].unsqueeze(1).to_broadcast([16, HD, TT])
                            sp.dma_start(r_t[:, m, :], src).then_inc(y_in, 16)

            @block.gpsimd
            def _(pool):
                pool.iota(iota16[:], pattern=[[1, E]], base=0, channel_multiplier=0,
                          allow_small_or_imprecise_dtypes=True).then_inc(consts3, 1)
                pool.memset(sel[:], 0.0).then_inc(consts3, 1)
                pool.wait_ge(consts3, 2)
                for part in range(3):
                    pool.affine_select(out=sel[:], in_=sel[:], compare_op=ALU.not_equal, fill=1.0, base=-part * E,
                                       pattern=[[-1, E], [0, P]], channel_multiplier=1).then_inc(consts3, 1)
                    pool.wait_ge(consts3, 3 + part)

            @block.scalar
            def _(act):
                with act.Fori(0, B) as b:
                    for half in range(2):
                        n = 2 * b + half + 1
                        act.wait_ge(var2, n)
                        act.activation(sd[:], sd[:], ACT.Sqrt).then_inc(sqrt2, 1)
                        at = b * T + half * TT
                        for c in range(DC):
                            act.wait_ge(h2_done, 2 * (n - 1) + c + 1)
                            act.activation(h2_hi[:, c, bass.ds(at, TT)], h2[:, c, :], ACT.Copy).then_inc(h2_hi_s, 1)
                        act.wait_ge(lg_ready, n)
                        act.activation(lg[:], lg[:], ACT.Exp).then_inc(lg_exp, 1)
                        act.wait_ge(cwt_full, n)
                        act.activation(cw_t[:, bass.ds(at, TT)], bank[5].bitcast(BF16)[0:CWR, 0:TT], ACT.Copy).then_inc(cwt_done, 1)

            @block.tensor
            def _(pe):
                with pe.Fori(0, B) as b:
                    for half in range(2):
                        n = 2 * b + half + 1
                        pe.wait_ge(yn_done, n + 1)
                        for j in range(TJ):
                            for m in range(DC):
                                last = pe.matmul(bank[j // 2][:, (j % 2) * D:(j % 2 + 1) * D], yn[:, m, j * P:(j + 1) * P],
                                                 wo_sb[:, m, :], start=(m == 0), stop=(m == DC - 1))
                        last.then_inc(att_full, 1)
                        pe.wait_ge(xn2_done, n)
                        for c in range(DC):
                            for j in range(TJ):
                                last = pe.transpose(bank[2 + c][:, j * P:(j + 1) * P], xn2[:, j, c * P:(c + 1) * P], ident[:])
                            last.then_inc(xt2_full, 1)
                        pe.wait_ge(h2_done, 2 * n)
                        for j in range(TJ):
                            for c in range(DC):
                                last = pe.matmul(bank[4][:, j * E:(j + 1) * E], h2[:, c, j * P:(j + 1) * P], wr_sb[:, c, :],
                                                 start=(c == 0), stop=(c == DC - 1))
                        last.then_inc(lg_full, 1)
                        pe.wait_ge(cwp_done, n)
                        pe.wait_ge(cwt_done, n)
                        settled(pe)
                        for j in range(TJ):
                            last = pe.transpose(bank[5].bitcast(BF16)[0:CWR, j * P:(j + 1) * P],
                                                cw_parts[:, j].rearrange("p a e -> p (a e)"), ident_b[:])
                        last.then_inc(cwt_full, 1)

            @block.vector
            def _(dve):
                dve.sem_inc(yn_done, 1)
                dve.sem_inc(cwt_done, 1)
                dve.wait_ge(l_in, 32)
                dve.reciprocal(r_sb[:], l_sb[:]).then_inc(l_recip, 1)
                dve.wait_ge(consts3, 1)
                with dve.Fori(0, B) as b:
                    for half in range(2):
                        n = 2 * b + half + 1
                        tile = b * TC + half * TJ
                        chain = Chain(dve, d3, NLINK3 * (n - 1))
                        link = chain.link
                        dve.wait_ge(y_in, 64 * n)
                        dve.tensor_tensor(out=yn[:], in0=y_t[:], in1=r_t[:], op=ALU.mult).then_inc(yn_done, 1)
                        dve.wait_ge(att_full, n)
                        link(dve.tensor_tensor(out=att[:], in0=psum[:, 0:2, :].rearrange("p a (c d) -> p (a c) d", c=2),
                                               in1=gate[:, 0, bass.ds(b, 1), :].to_broadcast([P, TJ, D]), op=ALU.mult))
                        link(dve.tensor_tensor(out=x_sb[:, bass.ds(tile, TJ), :], in0=x_sb[:, bass.ds(tile, TJ), :],
                                               in1=att[:], op=ALU.add))
                        layer_norm(dve, link, var2, sqrt2, n, tile, xn2).then_inc(xn2_done, 1)
                        for c in range(DC):
                            dve.wait_ge(xt2_full, 2 * (n - 1) + c + 1)
                            dve.tensor_scalar(h2[:, c, :], bank[2 + c][:], modc[:, b, 1, c, 0:1],
                                              modc[:, b, 1, c, 1:2], ALU.mult, ALU.add).then_inc(h2_done, 1)
                        for c in range(DC):
                            dve.wait_ge(h2_hi_s, 2 * (n - 1) + c + 1)
                            at = b * T + half * TT
                            dve.tensor_tensor(out=h2_lo[:, c, bass.ds(at, TT)], in0=h2[:, c, :],
                                              in1=h2_hi[:, c, bass.ds(at, TT)].bitcast(F32), op=ALU.subtract).then_inc(h2_lo_s, 1)
                        dve.wait_ge(lg_full, n)
                        logits = bank[4][:, 0:TJ * E].rearrange("p (j e) -> p j e", j=TJ)
                        link(dve.tensor_reduce(out=lmax[:], in_=logits, axis=AX.X, op=ALU.max))
                        dve.tensor_tensor(out=lg[:], in0=logits, in1=lmax[:].unsqueeze(2).to_broadcast([P, TJ, E]),
                                          op=ALU.subtract).then_inc(lg_ready, 1)
                        dve.wait_ge(lg_exp, n)
                        settled(dve)
                        for j in range(TJ):
                            ins = dve.max(top[:, j, :], lg[:, j, :])
                        link(ins)
                        settled(dve)
                        for j in range(TJ):
                            ins = dve.max_index(top_i[:, j, :], top[:, j, :], lg[:, j, :])
                        link(ins)
                        link(dve.tensor_copy(top_f[:], top_i[:]))
                        for j in range(TJ):
                            ins = dve.tensor_tensor(out=hit[:, j], in0=iota16[:].unsqueeze(1).to_broadcast([P, TOPK, E]),
                                                    in1=top_f[:, j, 0:TOPK].unsqueeze(2).to_broadcast([P, TOPK, E]),
                                                    op=ALU.is_equal)
                        link(ins)
                        link(dve.tensor_reduce(out=cw[:], in_=hit[:].rearrange("p j r e -> p j e r"), axis=AX.X, op=ALU.add))
                        link(dve.tensor_tensor(out=cw[:], in0=cw[:], in1=lg[:], op=ALU.mult))
                        link(dve.tensor_reduce(out=wsum[:], in_=cw[:], axis=AX.X, op=ALU.add))
                        link(dve.reciprocal(wsum[:], wsum[:]))
                        link(dve.tensor_scalar(wsum[:], wsum[:], float(TOPK), None, ALU.mult))
                        link(dve.tensor_tensor(out=cw[:], in0=cw[:], in1=wsum[:].unsqueeze(2).to_broadcast([P, TJ, E]),
                                               op=ALU.mult))
                        link(dve.tensor_copy(cw_parts[:, :, 0, :], cw[:]))
                        link(dve.tensor_tensor(out=cw_rest[:], in0=cw[:], in1=cw_parts[:, :, 0, :], op=ALU.subtract))
                        link(dve.tensor_copy(cw_parts[:, :, 1, :], cw_rest[:]))
                        dve.tensor_tensor(out=cw_parts[:, :, 2, :], in0=cw_rest[:], in1=cw_parts[:, :, 1, :],
                                          op=ALU.subtract).then_inc(cwp_done, 1)
                        dve.wait_ge(cwt_full, n)
                        assert chain.count == NLINK3, chain.count
        post.close()

        wl_hi = sb(moe, "wl_hi", [P, NLATE, WCOLS], F32R)
        wl_lo = sb(moe, "wl_lo", [P, NLATE, WCOLS], F32R)
        wl_raw = sb(moe, "wl_raw", [P, WCOLS], F32)
        mid = sb(moe, "mid", [P, 2, TT], F32)
        g_hi = sb(moe, "g_hi", [P, 2, TT], F32R)
        g_lo = sb(moe, "g_lo", [P, 2, TT], F32R)
        wl_in, wl_hi_s, wl_lo_s = sem("late_w_loaded"), sem("late_w_high"), sem("late_w_low")
        up_full, silu_done, mult_done, cw_full, cw_used = sem("up_full"), sem("silu_done"), sem("mult_done"), sem("cw_full"), sem("cw_used")
        ghi_done, glo_done, down_done = sem("g_high_done"), sem("g_low_done"), sem("down_done")
        y_read, fin_done, o_out, d4 = sem("y_read"), sem("out_ready"), sem("out_written"), sem("dve_chain4")

        def weights(e):
            return (w_hi[:, e, :], w_lo[:, e, :]) if e < NEARLY else (wl_hi[:, e - NEARLY, :], wl_lo[:, e - NEARLY, :])

        with nc.Block() as block:
            @block.sync
            def _(sp):
                for k in range(NLATE):
                    e = NEARLY + k
                    if k:
                        sp.wait_ge(wl_lo_s, k)
                    if e < E:
                        load_expert(sp, wl_raw[:], we1_in[e], we3_in[e], we2_in[e], wl_in)
                    else:
                        cols = slice((e - E) * H, (e - E + 1) * H)
                        load_expert(sp, wl_raw[:], ws1_in[:, cols], ws3_in[:, cols], ws2_in[cols, :], wl_in)
                with sp.Fori(0, B * T // TT) as t:
                    sp.wait_ge(fin_done, t + 2)
                    sp.dma_start(out_view[:, bass.ds(t * TJ, TJ), :], x_sb[:, bass.ds(t * TJ, TJ), :]).then_inc(o_out, 16)
                sp.wait_ge(o_out, 16 * (B * T // TT))

            @block.gpsimd
            def _(pool):
                for k in range(NLATE):
                    pool.wait_ge(wl_in, 48 * (k + 1))
                    pool.tensor_copy(wl_hi[:, k, :], wl_raw[:]).then_inc(wl_hi_s, 1)
                    pool.wait_ge(wl_hi_s, k + 1)
                    pool.tensor_tensor(out=wl_lo[:, k, :], in0=wl_raw[:], in1=wl_hi[:, k, :].bitcast(F32),
                                       op=ALU.subtract).then_inc(wl_lo_s, 1)

            @block.scalar
            def _(act):
                with act.Fori(0, B * T // TT) as t:
                    def high(e):
                        if e < E:
                            act.wait_ge(cw_used, E * t + e + 1 + 2)
                        else:
                            act.wait_ge(mult_done, NE * t + e + 1 + 2)
                        act.wait_ge(down_done, NE * t + e - 1 + 2)
                        act.activation(g_hi[:, e % 2, :], mid[:, e % 2, :], ACT.Copy).then_inc(ghi_done, 1)
                    for e in range(NE):
                        act.wait_ge(up_full, NE * t + e + 1)
                        act.wait_ge(glo_done, NE * t + e - 1 + 2)
                        if e == 0:
                            act.wait_ge(fin_done, t + 1)
                        act.activation(mid[:, e % 2, :], bank[e % 2][:], ACT.Silu).then_inc(silu_done, 1)
                        if e:
                            high(e - 1)
                    high(NE - 1)

            @block.tensor
            def _(pe):
                pe.sem_inc(down_done, 2)
                with pe.Fori(0, B * T // TT) as t:
                    at = t * TT

                    def up(e):
                        hi, lo = weights(e)
                        if e >= NEARLY:
                            pe.wait_ge(wl_lo_s, e - NEARLY + 1)
                        pe.wait_ge(silu_done, NE * t + e - 1 + 2)
                        pe.wait_ge(mult_done, NE * t + e - 1 + 2)
                        for m in range(2):
                            n = 0
                            for w, h in ((hi, h2_hi), (lo, h2_hi), (hi, h2_lo)):
                                for c in range(DC):
                                    col = c * 2 * H + m * H
                                    last = pe.matmul(bank[2 * m + e % 2][:], w[:, col:col + H], h[:, c, bass.ds(at, TT)],
                                                     start=(n == 0), stop=(n == 5))
                                    n += 1
                        last.then_inc(up_full, 1)
                        if e < E:
                            pe.wait_ge(cw_used, E * t + e - 1 + 2)
                            settled(pe)
                            pe.matmul(bank[4 + e % 2][:], sel[:, e, :], cw_t[:, bass.ds(at, TT)], start=True, stop=True)\
                              .then_inc(cw_full, 1)

                    def down(e):
                        hi, lo = weights(e)
                        pe.wait_ge(glo_done, NE * t + e + 1 + 2)
                        if e == 0:
                            pe.wait_ge(y_read, t + 1)
                        for g, w in ((g_hi, hi), (g_lo, hi), (g_hi, lo)):
                            for j in range(TJ):
                                first = e == 0 and g is g_hi and w is hi and j % 2 == 0
                                last = pe.matmul(bank[6 + j // 2][:, (j % 2) * D:(j % 2 + 1) * D],
                                                 g[:, e % 2, j * P:(j + 1) * P], w[:, W13:WCOLS],
                                                 start=first, stop=(e == NE - 1 and w is lo), skip_group_check=True)
                        last.then_inc(down_done, 1)

                    for e in range(NE):
                        up(e)
                        if e >= 2:
                            down(e - 2)
                    down(NE - 2)
                    down(NE - 1)

            @block.vector
            def _(dve):
                for s_, n in ((glo_done, 2), (silu_done, 2), (mult_done, 2), (cw_used, 2), (y_read, 1), (fin_done, 1)):
                    dve.sem_inc(s_, n)
                with dve.Fori(0, B) as b, dve.Fori(0, 2) as half:
                    t = 2 * b + half

                    def low(e):
                        dve.wait_ge(ghi_done, NE * t + e + 1)
                        dve.tensor_tensor(out=g_lo[:, e % 2, :], in0=mid[:, e % 2, :], in1=g_hi[:, e % 2, :].bitcast(F32),
                                          op=ALU.subtract).then_inc(glo_done, 1)
                    for e in range(NE):
                        m = mid[:, e % 2, :]
                        dve.wait_ge(silu_done, NE * t + e + 1 + 2)
                        ins = dve.tensor_tensor(out=m, in0=m, in1=bank[2 + e % 2][:], op=ALU.mult)
                        ins.then_inc(mult_done, 1)
                        if e < E:
                            dve.wait_ge(mult_done, NE * t + e + 1 + 2)
                            dve.wait_ge(cw_full, E * t + e + 1)
                            dve.tensor_tensor(out=m, in0=m, in1=bank[4 + e % 2][:], op=ALU.mult).then_inc(cw_used, 1)
                        if e:
                            low(e - 1)
                    low(NE - 1)
                    dve.wait_ge(down_done, NE * (t + 1) + 2)
                    sums = psum[:, 6:8, :].rearrange("p a (c d) -> p (a c) d", c=2)
                    out_tile = x_sb[:, bass.ds(t * TJ, TJ), :]
                    fin = mid[:].rearrange("p a (c d) -> p (a c) d", c=2)
                    ins = dve.tensor_tensor(out=fin, in0=sums, in1=gate[:, 1, bass.ds(b, 1), :].to_broadcast([P, TJ, D]), op=ALU.mult)
                    ins.then_inc(y_read, 1)
                    dve.wait_ge(y_read, t + 2)
                    dve.tensor_tensor(out=out_tile, in0=out_tile, in1=fin, op=ALU.add).then_inc(fin_done, 1)
        moe.close()


_INS = ["L0_attn_x", "L0_attn_wq", "L0_attn_wk", "L0_attn_wv", "L0_attn_wo", "L0_ffn_w_router", "L0_ffn_we1",
        "L0_ffn_we3", "L0_ffn_we2", "L0_ffn_ws1", "L0_ffn_ws3", "L0_ffn_ws2", "L0_c", "L0_wmod"]


def kernel(**inputs):
    import numpy as _np
    import concourse.bacc as _bacc
    from concourse import mybir as _mybir
    from concourse.bass_utils import run_bass_kernel_spmd as _run

    nc = _bacc.Bacc("TRN2", target_bir_lowering=False, num_devices=1)
    arrays, args = {}, []
    for name in _INS:
        a = _np.ascontiguousarray(inputs[name])
        arrays[f"in_{name}_dram"] = a
        args.append(nc.dram_tensor(f"in_{name}_dram", a.shape, _mybir.dt.from_np(a.dtype), kind="ExternalInput").ap())
    args.append(nc.dram_tensor("out_0_dram", (B, T, D), _mybir.dt.float32, kind="ExternalOutput").ap())
    block_kernel(nc, *args)
    r = _run(nc, [arrays], core_ids=[0])
    return r.results[0]["out_0_dram"]
```

```python
from contextlib import ExitStack

import concourse.bass as bass
from concourse import mybir

F32 = mybir.dt.float32
F32R = mybir.dt.float32r
BF16 = mybir.dt.bfloat16
U32 = mybir.dt.uint32
ALU = mybir.AluOpType
ACT = mybir.ActivationFunctionType
AX = mybir.AxisListType

P = 128
B, T, D = 2, 1024, 256
NH, NKV, HD = 32, 8, 8
REP = NH // NKV
DC = D // P
TT = 512
TJ = TT // P
NT = B * T // P
GROUPS = B * NKV
TC = T // P
E, H, HS, TOPK = 16, 128, 512, 4
NE = E + HS // H
NEARLY = 8
NLATE = NE - NEARLY
WCOLS = DC * 2 * H + D
W13 = DC * 2 * H
EPS = 1e-5
SCALE = HD ** -0.5
LEAST = -3.0e38
MASKED = -1.0e30
PROD = 4 * HD
STACK = PROD + 2

STEPS = [(0, c, c * P) for c in range(TC // 2)] + [(1, c, max(0, c - TC // 2) * P) for c in range(TC)]
NSTEP = len(STEPS)


def max_units():
    units = []
    for i in range(TC):
        n, key, part = i + 1, 0, 0
        while n >= 4:
            units += [(i, h, 1, key, 4 * P, part) for h in range(REP)]
            n, key, part = n - 4, key + 4 * P, part + 1
        if n >= 2:
            units += [(i, h, 2, key, 2 * P, part) for h in (0, 2)]
            n, key, part = n - 2, key + 2 * P, part + 1
        if n:
            units += [(i, 0, 4, key, P, part)]
    return units


UNITS = max_units()
NU = len(UNITS)
PARTS = 1 + max(u[5] for u in UNITS)
NB = 3
PER_STEP = NU // NSTEP
AHEAD = 2 * PER_STEP
LAG = 2
assert NU % NB == 0 and NU % NSTEP == 0 and NSTEP % (LAG + 1) == 0 and PER_STEP == 3


class Chain:

    def __init__(self, eng, sem, start):
        self.eng, self.sem, self.count, self.start = eng, sem, 0, start

    def link(self, ins):
        self.count += 1
        ins.then_inc(self.sem, 1)
        self.eng.wait_ge(self.sem, self.start + self.count)


def block_kernel(nc, x_in, wq_in, wk_in, wv_in, wo_in, wr_in, we1_in, we3_in, we2_in,
                 ws1_in, ws3_in, ws2_in, c_in, wmod_in, out):
    q_dram = nc.dram_tensor("q_parts", (2, GROUPS * REP * HD, T), F32, kind="Internal").ap()
    k_dram = nc.dram_tensor("k_parts", (2, GROUPS * HD, T), F32, kind="Internal").ap()
    y_dram = nc.dram_tensor("y_sums", (GROUPS, P, T), F32, kind="Internal").ap()
    r_dram = nc.dram_tensor("row_reciprocals", (B, NH, T), F32, kind="Internal").ap()

    x_view = x_in.rearrange("b (n p) d -> p (b n) d", p=P)
    out_view = out.rearrange("b (n p) d -> p (b n) d", p=P)

    whole = ExitStack()
    with whole:
        def sb(stack, name, shape, dt):
            return stack.enter_context(nc.sbuf_tensor(name, shape, dt))

        def sem(name):
            return whole.enter_context(nc.semaphore(name))

        psum = whole.enter_context(nc.psum_tensor("psum", [P, 8, 512], F32))
        bank = [psum[:, i, :] for i in range(8)]

        x_sb = sb(whole, "x_sb", [P, NT, D], F32)
        w_hi = sb(whole, "w_hi", [P, NEARLY, WCOLS], F32R)
        w_lo = sb(whole, "w_lo", [P, NEARLY, WCOLS], F32R)
        gate = sb(whole, "gate", [P, 2, B, D], F32)
        modc = sb(whole, "modc", [P, B, 2, DC, 2], F32)
        ident = sb(whole, "ident", [P, P], F32)
        ident_b = sb(whole, "ident_b", [P, P], BF16)
        wo_sb = sb(whole, "wo_sb", [P, DC, D], F32)
        wr_sb = sb(whole, "wr_sb", [P, DC, E], F32)
        stats = sb(whole, "stats", [P, NT, 6], F32)
        mv = sb(whole, "mv", [P, NT, 2], F32)
        sd = sb(whole, "sd", [P, NT], F32)
        rstd = sb(whole, "rstd", [P, NT], F32)

        def settled(eng):
            eng.sem_inc(passed, 1)

        passed = sem("passed")

        def moments(dve, link, tile):
            settled(dve)
            for j in range(TJ):
                ins = dve.bn_stats(stats[:, tile + j, :], x_sb[:, tile + j, :])
            link(ins)

        def deviations(dve, link, sqrt_ready, sqrt_done):
            settled(dve)
            for j in range(NT):
                ins = dve.bn_aggr(mv[:, j, :], stats[:, j, :])
            link(ins)
            dve.tensor_scalar(sd[:, :], mv[:, :, 1], EPS, None, ALU.add).then_inc(sqrt_ready, 1)
            dve.wait_ge(sqrt_done, 1)
            link(dve.reciprocal(rstd[:, :], sd[:, :]))

        def normalise(dve, tile, xn):
            for j in range(TJ):
                ins = dve.tensor_scalar(xn[:, j, :], x_sb[:, tile + j, :], mv[:, tile + j, 0:1],
                                        rstd[:, bass.ds(tile + j, 1)], ALU.subtract, ALU.mult)
            return ins

        attn = ExitStack()
        qa, qb = [[sb(attn, f"{n}{k}", [P, REP, T], F32R) for k in range(2)] for n in ("qa", "qb")]
        ka, kb = [[sb(attn, f"{n}{k}", [P, T], F32R) for k in range(2)] for n in ("ka", "kb")]
        v_all = sb(attn, "v_all", [P, GROUPS, TC, HD], F32)

        pro = ExitStack()
        wq_sb = sb(pro, "wq_sb", [P, DC, NH * HD], F32)
        wk_sb = sb(pro, "wk_sb", [P, DC, NKV * HD], F32)
        wv_sb = sb(pro, "wv_sb", [P, DC, NKV * HD], F32)
        wmod_sb = sb(pro, "wmod_sb", [P, DC, 6 * D], F32)
        c_sb = sb(pro, "c_sb", [P, DC, B], F32)
        c_rep = sb(pro, "c_rep", [P, DC, B, P], F32)
        g_sign = sb(pro, "g_sign", [P, 2, B, D], F32)
        g_size = sb(pro, "g_size", [P, 2, B, D], F32)
        xn = sb(pro, "xn", [P, 2, TJ, D], F32)
        h_t = sb(pro, "h_t", [P, 2, DC, TT], F32)
        w_hi_flat, w_lo_flat = [w[:].rearrange("p e n -> p (e n)") for w in (w_hi, w_lo)]
        q_parts = w_hi_flat[:, 0:4 * DC * TT].rearrange("p (k a m t) -> p k a m t", k=2, a=2, m=DC)
        k_parts = w_lo_flat[0:NKV * HD, 0:4 * TT].rearrange("p (k a t) -> p k a t", k=2, a=2)

        c_in_s, wmod_s, wqkv_s = sem("c_loaded"), sem("wmod_loaded"), sem("wqkv_loaded")
        x_s = [sem(f"x_loaded_{k}") for k in range(2 * B)]
        consts_s, c_silu, c_repd = sem("consts_ready"), sem("c_silu"), sem("c_repeated")
        modc_mm, gate_mm, mod_done = sem("modc_mm"), sem("gate_mm"), sem("mod_done")
        d1 = sem("dve_chain1")
        var1, sqrt1, xn1 = sem("var1_ready"), sem("sqrt1_done"), sem("xn1_ready")
        xt_full, ht_ready = sem("xt_full"), sem("ht_ready")
        q_full, k_full, v_full = sem("q_full"), sem("k_full"), sem("v_full")
        hi_done, lo_done, v_done = sem("qk_high_done"), sem("qk_low_done"), sem("v_done")
        qk_out = [sem(f"qk_out_{k}") for k in range(2)]
        OUTS1 = 16 * (2 * DC + 2)
        zeros_s = sem("stacks_zeroed")
        MODCOLS = [1, 0, 4, 3]
        QKV = DC + 1

        with nc.Block() as block:
            @block.sync
            def _(sp):
                sp.dma_start(c_sb[:, :, 0], c_in[0, :].rearrange("(c p) -> p c", p=P),
                             allow_slow_non_contiguous=True).then_inc(c_in_s, 16)
                sp.dma_start(c_sb[:, :, 1], c_in[1, :].rearrange("(c p) -> p c", p=P),
                             allow_slow_non_contiguous=True).then_inc(c_in_s, 16)
                for q in range(4):
                    sp.dma_start(x_sb[:, q * TJ:(q + 1) * TJ, :], x_view[:, q * TJ:(q + 1) * TJ, :]).then_inc(x_s[q], 16)
                sp.dma_start(wq_sb[:], wq_in.rearrange("(c p) n -> p c n", p=P)).then_inc(wqkv_s, 16)
                sp.dma_start(wk_sb[:], wk_in.rearrange("(c p) n -> p c n", p=P)).then_inc(wqkv_s, 16)
                sp.dma_start(wv_sb[:], wv_in.rearrange("(c p) n -> p c n", p=P)).then_inc(wqkv_s, 16)
                sp.dma_start(wo_sb[:], wo_in.rearrange("(c p) n -> p c n", p=P)).then_inc(wqkv_s, 16)
                sp.dma_start(wr_sb[:], wr_in.rearrange("(c p) n -> p c n", p=P)).then_inc(wqkv_s, 16)
                with sp.Fori(0, B) as b:
                    for half in range(2):
                        n = 2 * b + half + 1
                        toks = slice(half * TT, (half + 1) * TT)
                        for m in range(DC):
                            sp.wait_ge(lo_done, QKV * n + m + 1)
                            for part in range(2):
                                sp.dma_start(q_dram[part, bass.ds(b * NH * HD + m * P, P), toks],
                                             q_parts[:, half, part, m, :].bitcast(F32)).then_inc(qk_out[half], 16)
                        sp.wait_ge(lo_done, QKV * n + QKV)
                        for part in range(2):
                            sp.dma_start(k_dram[part, bass.ds(b * NKV * HD, NKV * HD), toks],
                                         k_parts[:, half, part, :].bitcast(F32)).then_inc(qk_out[half], 16)
                for half in range(2):
                    sp.wait_ge(qk_out[half], 16 + OUTS1 * B)

            @block.gpsimd
            def _(pool):
                pool.dma_start(wmod_sb[:], wmod_in.rearrange("(c p) n -> p c n", p=P)).then_inc(wmod_s, 16)
                pool.memset(ident[:], 0.0).then_inc(consts_s, 1)
                pool.memset(ident_b[:], 0.0).then_inc(consts_s, 1)
                pool.wait_ge(consts_s, 2)
                for m in (ident, ident_b):
                    pool.affine_select(out=m[:, :], in_=m[:, :], compare_op=ALU.not_equal, fill=1.0, base=0,
                                       pattern=[[-1, P]], channel_multiplier=1).then_inc(consts_s, 1)
                for tile in ka + kb + qa + qb:
                    pool.memset(tile[:].bitcast(F32), 0.0).then_inc(zeros_s, 1)

            @block.scalar
            def _(act):
                for half in range(2):
                    act.sem_inc(qk_out[half], 16)
                act.wait_ge(c_in_s, 32)
                act.activation(c_sb[:], c_sb[:], ACT.Silu).then_inc(c_silu, 1)
                act.wait_ge(var1, 1)
                act.activation(sd[:], sd[:], ACT.Sqrt).then_inc(sqrt1, 1)
                with act.Fori(0, B) as b:
                    for half in range(2):
                        n = 2 * b + half + 1
                        act.wait_ge(qk_out[half], OUTS1 * b + 16)
                        for m in range(DC):
                            act.wait_ge(q_full, DC * (n - 1) + m + 1)
                            act.activation(q_parts[:, half, 0, m, :], bank[2 + m][:], ACT.Copy).then_inc(hi_done, 1)
                        act.wait_ge(k_full, n)
                        act.activation(k_parts[:, half, 0, :], bank[4][0:NKV * HD, :], ACT.Copy).then_inc(hi_done, 1)

            @block.tensor
            def _(pe):
                pe.wait_ge(c_silu, 1)
                pe.wait_ge(wmod_s, 16)
                for k, which in enumerate(MODCOLS):
                    for c in range(DC):
                        for kc in range(DC):
                            last = pe.matmul(bank[5][:, (k * DC + c) * B:(k * DC + c + 1) * B],
                                             wmod_sb[:, kc, which * D + c * P:which * D + (c + 1) * P],
                                             c_sb[:, kc, :], start=(kc == 0), stop=(kc == DC - 1))
                last.then_inc(modc_mm, 1)
                pe.wait_ge(consts_s, 4)
                pe.wait_ge(wqkv_s, 16 * 5)
                with pe.Fori(0, B) as b:
                    for half in range(2):
                        n = 2 * b + half + 1
                        pe.wait_ge(xn1, n)
                        for c in range(DC):
                            for j in range(TJ):
                                last = pe.transpose(bank[6 * half + c][:, j * P:(j + 1) * P],
                                                    xn[:, half, j, c * P:(c + 1) * P], ident[:])
                            last.then_inc(xt_full, 1)
                    for half in range(2):
                        n = 2 * b + half + 1
                        pe.wait_ge(ht_ready, DC * n)
                        for m in range(DC):
                            pe.wait_ge(lo_done, QKV * (n - 1) + m + 1)
                            for kc in range(DC):
                                last = pe.matmul(bank[2 + m][:], wq_sb[:, kc, m * P:(m + 1) * P], h_t[:, half, kc, :],
                                                 start=(kc == 0), stop=(kc == DC - 1))
                            last.then_inc(q_full, 1)
                        pe.wait_ge(lo_done, QKV * (n - 1) + QKV)
                        for kc in range(DC):
                            last = pe.matmul(bank[4][0:NKV * HD, :], wk_sb[:, kc, :], h_t[:, half, kc, :],
                                             start=(kc == 0), stop=(kc == DC - 1))
                        last.then_inc(k_full, 1)
                        pe.wait_ge(v_done, n)
                        for j in range(TJ):
                            for kc in range(DC):
                                last = pe.matmul(bank[5][:, j * NKV * HD:(j + 1) * NKV * HD],
                                                 h_t[:, half, kc, j * P:(j + 1) * P], wv_sb[:, kc, :],
                                                 start=(kc == 0), stop=(kc == DC - 1))
                        last.then_inc(v_full, 1)
                pe.wait_ge(c_repd, 1)
                for g, which in enumerate((2, 5)):
                    for b in range(B):
                        for kc in range(DC):
                            last = pe.matmul(bank[6 + g][:, b * D:(b + 1) * D], c_rep[:, kc, b, :],
                                             wmod_sb[:, kc, which * D:(which + 1) * D],
                                             start=(kc == 0), stop=(kc == DC - 1))
                last.then_inc(gate_mm, 1)

            @block.vector
            def _(dve):
                dve.sem_inc(v_done, 1)
                dve.sem_inc(lo_done, QKV)
                chain = Chain(dve, d1, 0)
                for q in range(2 * B):
                    dve.wait_ge(x_s[q], 16)
                    moments(dve, chain.link, q * TJ)
                dve.wait_ge(c_silu, 1)
                dve.tensor_copy(c_rep[:], c_sb[:].unsqueeze(3).to_broadcast([P, DC, B, P])).then_inc(c_repd, 1)
                deviations(dve, chain.link, var1, sqrt1)
                dve.wait_ge(modc_mm, 1)
                for norm in range(2):
                    cols = bank[5][:, 8 * norm:8 * norm + 8].rearrange("p (k c b) -> p b c k", k=2, c=DC)
                    ins = dve.tensor_copy(modc[:, :, norm, :, :], cols)
                chain.link(ins)
                dve.tensor_scalar(modc[:, :, :, :, 0], modc[:, :, :, :, 0], 1.0, None, ALU.add).then_inc(mod_done, 1)
                dve.wait_ge(mod_done, 1)
                with dve.Fori(0, B) as b:
                    for half in range(2):
                        normalise(dve, b * TC + half * TJ, xn[:, half]).then_inc(xn1, 1)
                    for half in range(2):
                        n = 2 * b + half + 1
                        for c in range(DC):
                            dve.wait_ge(xt_full, DC * (n - 1) + c + 1)
                            dve.tensor_scalar(h_t[:, half, c, :], bank[6 * half + c][:], modc[:, b, 0, c, 0:1],
                                              modc[:, b, 0, c, 1:2], ALU.mult, ALU.add).then_inc(ht_ready, 1)
                    for half in range(2):
                        n = 2 * b + half + 1
                        for m in range(DC):
                            dve.wait_ge(hi_done, QKV * (n - 1) + m + 1)
                            dve.tensor_tensor(out=q_parts[:, half, 1, m, :], in0=bank[2 + m][:],
                                              in1=q_parts[:, half, 0, m, :].bitcast(F32), op=ALU.subtract).then_inc(lo_done, 1)
                        dve.wait_ge(hi_done, QKV * n)
                        dve.tensor_tensor(out=k_parts[:, half, 1, :], in0=bank[4][0:NKV * HD, :],
                                          in1=k_parts[:, half, 0, :].bitcast(F32), op=ALU.subtract).then_inc(lo_done, 1)
                        dve.wait_ge(v_full, n)
                        dve.tensor_copy(v_all[:, bass.ds(b * NKV, NKV), half * TJ:(half + 1) * TJ, :]
                                        .rearrange("p g j d -> p j g d"),
                                        bank[5][:, 0:TJ * NKV * HD].rearrange("p (j g d) -> p j g d", j=TJ, g=NKV))\
                           .then_inc(v_done, 1)
                dve.wait_ge(gate_mm, 1)
                rows = psum[:, 6:8, :].rearrange("p g (b d) -> p g b d", b=B)
                dve.tensor_scalar(g_sign[:], rows, 0.0, 2.0, ALU.is_ge, ALU.mult)
                chain.link(dve.tensor_scalar(g_size[:], rows, -1.0, 0.25, ALU.mult, ALU.max))
                chain.link(dve.tensor_tensor(out=g_size[:], in0=g_size[:], in1=rows, op=ALU.max))
                for g in range(2):
                    ins = dve.scalar_tensor_tensor(out=gate[:, g, :, :], in0=g_sign[:, g, :, :], scalar=-1.0,
                                                   in1=g_size[:, g, :, :], op0=ALU.add, op1=ALU.mult)
                chain.link(ins)
                dve.tensor_scalar(gate[:, 1, :, :], gate[:, 1, :, :], 1.0 / (TOPK + 1), None, ALU.mult)
        pro.close()

        core = ExitStack()
        probs = sb(core, "probs", [P, LAG + 1, REP, TT], F32)
        v_aug = sb(core, "v_aug", [P, 2, TC, 32], F32)
        y_sb = sb(core, "y_sb", [P, 2, TT], F32)
        max_parts = sb(core, "max_parts", [P, REP, TC, PARTS], F32)
        neg_max = sb(core, "neg_max", [P, 2, REP * TC], F32)
        neg_max_f = sb(core, "neg_max_f", [P, REP * TC], F32)
        neg_max_t = sb(core, "neg_max_t", [2 * REP * TC, P], F32)
        w_raw = sb(core, "w_raw", [P, 2, WCOLS], F32)
        causal = sb(core, "causal", [P, P], BF16)
        ident4 = sb(core, "ident4", [P, REP, P], BF16)

        unit_bank, sum_bank = (4, 5, 6), 7
        qa_in, qb_in, raw_in = [[sem(f"{n}_{k}") for k in range(2)] for n in ("qa_loaded", "qb_loaded", "raw_loaded")]
        row_in, y_out = [[sem(f"{n}_{k}") for k in range(2)] for n in ("max_rows_loaded", "sums_out")]
        consts2, v_aug_s, parts_set = sem("consts2_ready"), sem("v_aug_ready"), sem("max_parts_set")
        unit_full, unit_free = sem("unit_full"), sem("unit_free")
        negm_done, negt_full, negt_done = sem("neg_max_done"), sem("neg_max_t_full"), sem("neg_max_t_done")
        st_full, p_full, p_masked, pv_done = sem("scores_full"), sem("probs_full"), sem("probs_masked"), sem("pv_done")
        y_done, hi2, lo2, d2 = sem("sums_copied"), sem("w_high_done"), sem("w_low_done"), sem("dve_chain2")
        LOADS = 16 * 8
        NDIAG = TC

        def wait_if(eng, s, value):
            if not isinstance(value, int) or value > 0:
                eng.wait_ge(s, value)

        def load_stacks(sp, group, q_tile, k_tile, par, loaded):
            for block8 in range(4):
                row = HD * block8
                q_rows = q_dram[block8 % 2, bass.ds(group * REP * HD, REP * HD), :]
                sp.dma_start(q_tile[par][row:row + HD].bitcast(F32), q_rows.rearrange("(h d) t -> d h t", h=REP))\
                  .then_inc(loaded[par], 16)
                sp.dma_start(k_tile[par][row:row + HD, :].bitcast(F32), k_dram[block8 // 2, bass.ds(group * HD, HD), :])\
                  .then_inc(loaded[par], 16)

        def load_expert(eng, raw, w1, w3, w2, loaded):
            cols = raw[:, 0:W13].rearrange("p (c w h) -> p c w h", c=DC, w=2)
            eng.dma_start(cols[:, :, 0, :], w1.rearrange("(c p) h -> p c h", p=P)).then_inc(loaded, 16)
            eng.dma_start(cols[:, :, 1, :], w3.rearrange("(c p) h -> p c h", p=P)).then_inc(loaded, 16)
            eng.dma_start(raw[:, W13:WCOLS], w2).then_inc(loaded, 16)

        def periods(eng, period):
            period(0, 0)
            period(0, 1)
            with eng.Fori(1, NEARLY // 2) as it:
                period(it, 0)
                period(it, 1)
            with eng.Fori(NEARLY // 2, GROUPS // 2 - 1) as it:
                period(it, 0, weights=False)
                period(it, 1, weights=False)
            period(GROUPS // 2 - 1, 0, last=1)
            period(GROUPS // 2 - 1, 1, last=2)

        def ahead(it, par, s, last):
            for u in range(PER_STEP * s + AHEAD, PER_STEP * (s + 1) + AHEAD):
                if u < NU and last < 2:
                    yield (it + par, 1 - par, u)
                elif u >= NU and last < 1:
                    yield (it + 1, par, u - NU)

        with nc.Block() as block:
            @block.sync
            def _(sp):
                def rows_in(it, par):
                    sp.wait_ge(negt_done, 2 * it + par + 1)
                    for part in range(2):
                        row = PROD + part
                        sp.dma_start(qb[par][row:row + 1].bitcast(F32),
                                     neg_max_t[part * REP * TC:(part + 1) * REP * TC, :]).then_inc(row_in[par], 16)

                def sums_out(group, half):
                    sp.wait_ge(y_done, 2 * group + half + 1)
                    sp.dma_start(y_dram[group, :, half * TT:(half + 1) * TT], y_sb[:, half, :]).then_inc(y_out[half], 16)

                def period(it, par, last=0, weights=True):
                    group = 2 * it + par
                    if last < 2:
                        wait_if(sp, st_full, 2 * NSTEP * group)
                        load_stacks(sp, group + 1, qb, kb, 1 - par, qb_in)
                    if last < 1:
                        sp.wait_ge(unit_full, NU * (group + 1))
                        load_stacks(sp, group + 2, qa, ka, par, qa_in)
                    if weights and last < 1:
                        wait_if(sp, lo2, group - 1)
                        load_expert(sp, w_raw[:, par, :], we1_in[group], we3_in[group], we2_in[group], raw_in[par])
                    if not (isinstance(group, int) and group == 0):
                        sums_out(group - 1, 1)
                    sums_out(group, 0)
                    if last < 2:
                        rows_in(it + par, 1 - par)

                load_stacks(sp, 0, qa, ka, 0, qa_in)
                load_stacks(sp, 0, qb, kb, 0, qb_in)
                load_stacks(sp, 1, qa, ka, 1, qa_in)
                rows_in(0, 0)
                periods(sp, period)
                sums_out(GROUPS - 1, 1)
                for k in range(2):
                    sp.wait_ge(y_out[k], 16 * GROUPS)

            @block.gpsimd
            def _(pool):
                pool.memset(causal[:], 0.0).then_inc(consts2, 1)
                pool.memset(ident4[:], 0.0).then_inc(consts2, 1)
                pool.memset(v_aug[:], 1.0).then_inc(consts2, 1)
                pool.wait_ge(consts2, 3)
                pool.affine_select(out=causal[:, :], in_=causal[:, :], compare_op=ALU.is_ge, fill=MASKED, base=0,
                                   pattern=[[1, P]], channel_multiplier=-1).then_inc(consts2, 1)
                pool.affine_select(out=ident4[:], in_=ident4[:], compare_op=ALU.not_equal, fill=1.0, base=0,
                                   pattern=[[0, REP], [-1, P]], channel_multiplier=1).then_inc(consts2, 1)

                def values(group, par):
                    pool.tensor_copy(v_aug[:, par, :, 0:HD], v_all[:, group, :, :]).then_inc(v_aug_s, 1)

                def period(it, par, last=0, weights=True):
                    group = 2 * it + par
                    for s, (half, c, off) in enumerate(STEPS):
                        if c >= half * (TC // 2):
                            pool.wait_ge(p_full, 2 * NSTEP * group + 2 * s + 2)
                            tile = probs[:, s % (LAG + 1), :, off:off + P]
                            settled(pool)
                            pool.affine_select(out=tile, in_=tile, compare_op=ALU.is_ge, fill=0.0, base=0,
                                               pattern=[[0, REP], [1, P]], channel_multiplier=-1).then_inc(p_masked, 1)
                        if s == 3 and last < 2:
                            wait_if(pool, pv_done, NSTEP * group)
                            values(group + 1, 1 - par)
                        if s == 4 and weights and last < 1:
                            pool.wait_ge(hi2, group + 1)
                            pool.tensor_tensor(out=w_lo[:, group, :], in0=w_raw[:, par, :],
                                               in1=w_hi[:, group, :].bitcast(F32), op=ALU.subtract).then_inc(lo2, 1)

                values(0, 0)
                periods(pool, period)

            @block.scalar
            def _(act):
                def turned(it, par):
                    group = 2 * it + par
                    act.wait_ge(negt_full, group + 1)
                    wait_if(act, row_in[1 - par], 32 * (it + par))
                    act.activation(neg_max_t[:], bank[unit_bank[0]][0:2 * REP * TC, 0:P], ACT.Copy).then_inc(negt_done, 1)

                def sums(group, half):
                    act.wait_ge(pv_done, NSTEP * group + (TC // 2, NSTEP)[half])
                    wait_if(act, y_out[half], 16 * group)
                    act.activation(y_sb[:, half, :], bank[sum_bank][:, :], ACT.Copy).then_inc(y_done, 1)

                def period(it, par, last=0, weights=True):
                    group = 2 * it + par
                    for s, (half, c, off) in enumerate(STEPS):
                        wait_if(act, pv_done, NSTEP * group + s - LAG)
                        for pair in range(2):
                            act.wait_ge(st_full, 2 * NSTEP * group + 2 * s + pair + 1)
                            act.activation(probs[:, s % (LAG + 1), 2 * pair:2 * pair + 2, off:TT],
                                           psum[:, 2 * pair:2 * pair + 2, off:TT], ACT.Exp, scale=SCALE).then_inc(p_full, 1)
                        if s == 1 and not (isinstance(group, int) and group == 0):
                            sums(group - 1, 1)
                        if s == TC // 2 + LAG - 1:
                            sums(group, 0)
                        if s == 3 and weights and last < 1:
                            act.wait_ge(raw_in[par], 48 * (it + 1))
                            act.activation(w_hi[:, group, :], w_raw[:, par, :], ACT.Copy).then_inc(hi2, 1)
                        if s == NSTEP - 2 and last < 2:
                            turned(it + par, 1 - par)

                turned(0, 0)
                periods(act, period)
                sums(GROUPS - 1, 1)

            @block.tensor
            def _(pe):
                def unit(it, par, u):
                    i, h0, nh, key, w, _ = UNITS[u]
                    group, bk = 2 * it + par, bank[unit_bank[u % NB]]
                    if u == 0:
                        pe.wait_ge(qa_in[par], LOADS * (it + 1))
                    wait_if(pe, unit_free, NU * group + u - NB + 1)
                    if u == NB:
                        wait_if(pe, negt_done, group)
                    diag = key + w == (i + 1) * P
                    for k in range(nh):
                        last = pe.matmul(bk[:, k * w:(k + 1) * w], qa[par][:, h0 + k, i * P:(i + 1) * P],
                                         ka[par][:, key:key + w], start=(k == 0),
                                         stop=(k == nh - 1 and not diag), skip_group_check=True)
                    if diag:
                        last = pe.matmul(bk[:, 0:nh * w].rearrange("p (k w) -> p k w", k=nh)[:, :, w - P:w],
                                         causal[:], ident4[:, 0:nh, :], start=False, stop=True, skip_group_check=True)
                    last.then_inc(unit_full, 1)

                def turn(it, par, followed):
                    group = 2 * it + par
                    pe.wait_ge(negm_done, group + 1)
                    pe.wait_ge(unit_free, NU * (group + 1) + followed)
                    settled(pe)
                    pe.transpose(bank[unit_bank[0]][0:2 * REP * TC, 0:P],
                                 neg_max[:].rearrange("p a n -> p (a n)"), ident[:]).then_inc(negt_full, 1)

                def scores(it, par, s, pair):
                    half, c, off = STEPS[s]
                    group = 2 * it + par
                    if s == 0 and pair == 0:
                        pe.wait_ge(qb_in[par], LOADS * (it + 1))
                        pe.wait_ge(row_in[par], 32 * (it + 1))
                    wait_if(pe, p_full, 2 * NSTEP * group + 2 * s + pair - 1)
                    for h in (2 * pair, 2 * pair + 1):
                        last = pe.matmul(bank[h][:, off:TT], kb[par][:, c * P:(c + 1) * P],
                                         qb[par][:, h, half * TT + off:(half + 1) * TT],
                                         start=True, stop=True)
                    last.then_inc(st_full, 1)

                def product(it, par, s):
                    half, c, off = STEPS[s]
                    group = 2 * it + par
                    if s == 0:
                        pe.wait_ge(v_aug_s, group + 1)
                    if c == 0:
                        wait_if(pe, y_done, 2 * group + half)
                    pe.wait_ge(p_full, 2 * NSTEP * group + 2 * s + 2)
                    if c >= half * (TC // 2):
                        pe.wait_ge(p_masked, NDIAG * group + c + 1)
                    for h in range(REP):
                        last = pe.matmul(bank[sum_bank][32 * h:32 * h + 32, off:TT], v_aug[:, par, c, :],
                                         probs[:, s % (LAG + 1), h, off:TT], start=(c == 0),
                                         stop=(c == (TC // 2, TC)[half] - 1), skip_group_check=True)
                    last.then_inc(pv_done, 1)

                def period(it, par, last=0, weights=True):
                    for s in range(NSTEP):
                        units = list(ahead(it, par, s, last))
                        if s == NSTEP - 1 and last < 2:
                            turn(it + par, 1 - par, followed=1 if last == 0 else 0)
                        for k in range(PER_STEP):
                            if k < 2:
                                scores(it, par, s, k)
                            elif s >= LAG:
                                product(it, par, s - LAG)
                            elif par == 1:
                                product(it, 0, s - LAG + NSTEP)
                            elif not isinstance(it, int) or it > 0:
                                product(it - 1, 1, s - LAG + NSTEP)
                            if k < len(units):
                                unit(*units[k])

                pe.wait_ge(consts2, 5)
                pe.wait_ge(parts_set, 3)
                for u in range(NU):
                    unit(0, 0, u)
                for u in range(AHEAD):
                    if u == NB:
                        turn(0, 0, followed=1)
                    unit(0, 1, u)
                periods(pe, period)
                for s in range(NSTEP - LAG, NSTEP):
                    product(GROUPS // 2 - 1, 1, s)

            @block.vector
            def _(dve):
                def unit(it, par, u):
                    i, h0, nh, key, w, part = UNITS[u]
                    group = 2 * it + par
                    dve.wait_ge(unit_full, NU * group + u + 1)
                    dve.tensor_reduce(out=max_parts[:, h0:h0 + nh, i, part],
                                      in_=bank[unit_bank[u % NB]][:, 0:nh * w].rearrange("p (k w) -> p k w", k=nh),
                                      axis=AX.X, op=ALU.max).then_inc(unit_free, 1)
                    if u == NU - 1:
                        dve.wait_ge(unit_free, NU * (group + 1))
                        wait_if(dve, negm_done, group)
                        chain = Chain(dve, d2, 2 * group)
                        chain.link(dve.tensor_reduce(out=neg_max_f[:], in_=max_parts[:].rearrange("p h i a -> p (h i) a"),
                                                     axis=AX.X, op=ALU.max, negate=True))
                        wait_if(dve, negt_full, group)
                        chain.link(dve.tensor_copy(neg_max[:, 0, :].bitcast(F32R), neg_max_f[:]))
                        dve.tensor_tensor(out=neg_max[:, 1, :].bitcast(F32R), in0=neg_max_f[:], in1=neg_max[:, 0, :],
                                          op=ALU.subtract).then_inc(negm_done, 1)

                def period(it, par, last=0, weights=True):
                    for s in range(NSTEP):
                        for at in ahead(it, par, s, last):
                            unit(*at)

                dve.memset(max_parts[:], LEAST).then_inc(parts_set, 1)
                for par in range(2):
                    dve.memset(kb[par][PROD:STACK, :].bitcast(F32), 1.0).then_inc(parts_set, 1)
                dve.wait_ge(parts_set, 3)
                for u in range(NU):
                    unit(0, 0, u)
                for u in range(AHEAD):
                    unit(0, 1, u)
                periods(dve, period)
        core.close()
        attn.close()

        moe = ExitStack()
        h2_hi = sb(moe, "h2_hi", [P, DC, B * T], F32R)
        h2_lo = sb(moe, "h2_lo", [P, DC, B * T], F32R)
        CWR = 3 * E
        cw_t = sb(moe, "cw_t", [CWR, B * T], BF16)
        sel = sb(moe, "sel", [CWR, E, P], BF16)

        post = ExitStack()
        l_sb = sb(post, "l_sb", [P, B, T // 4], F32)
        y_t = sb(post, "y_t", [P, 2, DC, TT], F32)
        r_t = sb(post, "r_t", [P, 2, DC, TT], F32)
        att = sb(post, "att", [P, TJ, D], F32)
        xn2 = sb(post, "xn2", [P, 2, TJ, D], F32)
        h2 = sb(post, "h2", [P, 2, DC, TT], F32)
        iota16 = sb(post, "iota16", [P, E], F32)
        lg = sb(post, "lg", [P, NT, E], F32)
        lmax = sb(post, "lmax", [P, NT], F32)
        top = sb(post, "top", [P, NT, 8], F32)
        top_i = sb(post, "top_i", [P, NT, 8], U32)
        top_f = sb(post, "top_f", [P, NT, 8], F32)
        hit = sb(post, "hit", [P, NT, TOPK, E], F32)
        cw = sb(post, "cw", [P, NT, E], F32)
        cw_rest = sb(post, "cw_rest", [P, NT, E], F32)
        wsum = sb(post, "wsum", [P, NT], F32)
        cw_parts = sb(post, "cw_parts", [P, NT, 3, E], BF16)

        l_recip, r_out = sem("l_reciprocal"), sem("r_out")
        l_in = [sem(f"l_loaded_{b}") for b in range(B)]
        y_in = [sem(f"y_loaded_{k}") for k in range(2)]
        yn_done, att_full, att_done = sem("yn_done"), sem("att_full"), sem("att_gated")
        var2, sqrt2, xn2_done = sem("var2_ready"), sem("sqrt2_done"), sem("xn2_done")
        xt2_full, h2_done, h2_hi_s, h2_lo_s = sem("xt2_full"), sem("h2_done"), sem("h2_high_done"), sem("h2_low_done")
        lg_full, lg_ready, lg_exp, cwp_done = sem("logits_full"), sem("logits_ready"), sem("logits_exp"), sem("cw_parts_done")
        cwt_full, consts3, d3 = sem("cw_t_full"), sem("consts3_ready"), sem("dve_chain3")
        NLINK3 = 2
        lg_bank, cwt_bank = 4, (5, 6)
        with nc.Block() as block:
            @block.sync
            def _(sp):
                for b in range(B):
                    rows = y_dram[b * NKV:(b + 1) * NKV].rearrange("g (h r) (q t) -> g h r q t", r=32, q=4)
                    sp.dma_start(l_sb[:, b, :], rows[:, :, HD, :, :]).then_inc(l_in[b], 16)
                for b in range(B):
                    sp.wait_ge(l_recip, b + 1)
                    sp.dma_start(r_dram[b].rearrange("n (q t) -> (n q) t", q=4), l_sb[:, b, :]).then_inc(r_out, 16)
                sp.wait_ge(r_out, 16 * B)
                with sp.Fori(0, B) as b:
                    for half in range(2):
                        toks = slice(half * TT, (half + 1) * TT)
                        sp.wait_ge(att_full, 2 * b + half + 1)
                        for m in range(DC):
                            src = r_dram[b, 16 * m:16 * m + 16, toks].unsqueeze(1).to_broadcast([16, HD, TT])
                            sp.dma_start(r_t[:, half, m, :], src).then_inc(y_in[half], 16)
                            src = y_dram[bass.ds(b * NKV + 4 * m, 4), :, toks].rearrange("g (h r) t -> g h r t", r=32)
                            sp.dma_start(y_t[:, half, m, :], src[:, :, 0:HD, :]).then_inc(y_in[half], 16)

            @block.gpsimd
            def _(pool):
                pool.iota(iota16[:], pattern=[[1, E]], base=0, channel_multiplier=0,
                          allow_small_or_imprecise_dtypes=True).then_inc(consts3, 1)
                pool.memset(sel[:], 0.0).then_inc(consts3, 1)
                pool.wait_ge(consts3, 2)
                for part in range(3):
                    pool.affine_select(out=sel[:], in_=sel[:], compare_op=ALU.not_equal, fill=1.0, base=-part * E,
                                       pattern=[[-1, E], [0, P]], channel_multiplier=1).then_inc(consts3, 1)
                    pool.wait_ge(consts3, 3 + part)
                with pool.Fori(0, B) as b:
                    for half in range(2):
                        pool.wait_ge(y_in[half], 64 * (b + 1))
                        pool.tensor_tensor(out=y_t[:, half], in0=y_t[:, half], in1=r_t[:, half], op=ALU.mult)\
                            .then_inc(yn_done, 1)
                with pool.Fori(0, B) as b:
                    for half in range(2):
                        toks = bass.ds(b * T + half * TT, TT)
                        pool.wait_ge(h2_hi_s, DC * (2 * b + half + 1))
                        pool.tensor_tensor(out=h2_lo[:, :, toks], in0=h2[:, half], in1=h2_hi[:, :, toks].bitcast(F32),
                                           op=ALU.subtract).then_inc(h2_lo_s, 1)

            @block.scalar
            def _(act):
                act.wait_ge(var2, 1)
                act.activation(sd[:], sd[:], ACT.Sqrt).then_inc(sqrt2, 1)
                with act.Fori(0, B) as b:
                    for half in range(2):
                        n = 2 * b + half + 1
                        for c in range(DC):
                            act.wait_ge(h2_done, DC * (n - 1) + c + 1)
                            act.activation(h2_hi[:, c, bass.ds(b * T + half * TT, TT)], h2[:, half, c, :], ACT.Copy)\
                               .then_inc(h2_hi_s, 1)
                act.wait_ge(lg_ready, 1)
                act.activation(lg[:], lg[:], ACT.Exp).then_inc(lg_exp, 1)
                for b in range(B):
                    act.wait_ge(cwt_full, b + 1)
                    act.activation(cw_t[:, b * T:(b + 1) * T], bank[cwt_bank[b]].bitcast(BF16)[0:CWR, 0:T], ACT.Copy)

            @block.tensor
            def _(pe):
                pe.sem_inc(att_full, 2)
                pe.sem_inc(lg_full, 2)
                with pe.Fori(0, B) as b:
                    for half in range(2):
                        n = 2 * b + half + 1
                        pe.wait_ge(yn_done, n)
                        pe.wait_ge(att_done, n)
                        for j in range(TJ):
                            for m in range(DC):
                                last = pe.matmul(bank[2 * half + j // 2][:, (j % 2) * D:(j % 2 + 1) * D],
                                                 y_t[:, half, m, j * P:(j + 1) * P],
                                                 wo_sb[:, m, :], start=(m == 0), stop=(m == DC - 1))
                        last.then_inc(att_full, 1)
                with pe.Fori(0, B) as b:
                    for half in range(2):
                        pe.wait_ge(xn2_done, 2 * b + half + 1)
                        for c in range(DC):
                            for j in range(TJ):
                                last = pe.transpose(bank[2 * half + c][:, j * P:(j + 1) * P],
                                                    xn2[:, half, j, c * P:(c + 1) * P], ident[:])
                            last.then_inc(xt2_full, 1)
                    for half in range(2):
                        pe.wait_ge(h2_done, DC * (2 * b + half + 1))
                        for j in range(TJ):
                            for c in range(DC):
                                last = pe.matmul(bank[lg_bank][:, bass.ds((b * TC + half * TJ + j) * E, E)],
                                                 h2[:, half, c, j * P:(j + 1) * P], wr_sb[:, c, :],
                                                 start=(c == 0), stop=(c == DC - 1))
                        last.then_inc(lg_full, 1)
                pe.wait_ge(cwp_done, 1)
                for b in range(B):
                    for j in range(TC):
                        last = pe.transpose(bank[cwt_bank[b]].bitcast(BF16)[0:CWR, j * P:(j + 1) * P],
                                            cw_parts[:, b * TC + j].rearrange("p a e -> p (a e)"), ident_b[:])
                    last.then_inc(cwt_full, 1)

            @block.vector
            def _(dve):
                dve.sem_inc(att_done, 2)
                dve.sem_inc(h2_lo_s, 2)
                for b in range(B):
                    dve.wait_ge(l_in[b], 16)
                    dve.reciprocal(l_sb[:, b, :], l_sb[:, b, :]).then_inc(l_recip, 1)
                with dve.Fori(0, B) as b:
                    for half in range(2):
                        n = 2 * b + half + 1
                        tile = b * TC + half * TJ
                        chain = Chain(dve, d3, NLINK3 * (n - 1))
                        dve.wait_ge(att_full, n + 2)
                        dve.tensor_tensor(out=att[:], in0=psum[:, 2 * half:2 * half + 2, :].rearrange("p a (c d) -> p (a c) d", c=2),
                                          in1=gate[:, 0, bass.ds(b, 1), :].to_broadcast([P, TJ, D]), op=ALU.mult)\
                           .then_inc(att_done, 1)
                        dve.wait_ge(att_done, n + 2)
                        chain.link(dve.tensor_tensor(out=x_sb[:, bass.ds(tile, TJ), :], in0=x_sb[:, bass.ds(tile, TJ), :],
                                                     in1=att[:], op=ALU.add))
                        moments(dve, chain.link, tile)
                        assert chain.count == NLINK3
                chain = Chain(dve, d3, NLINK3 * 2 * B)
                link = chain.link
                deviations(dve, link, var2, sqrt2)
                with dve.Fori(0, B) as b:
                    for half in range(2):
                        normalise(dve, b * TC + half * TJ, xn2[:, half]).then_inc(xn2_done, 1)
                    for half in range(2):
                        n = 2 * b + half + 1
                        dve.wait_ge(h2_lo_s, n)
                        dve.wait_ge(lg_full, n)
                        for c in range(DC):
                            dve.wait_ge(xt2_full, DC * (n - 1) + c + 1)
                            dve.tensor_scalar(h2[:, half, c, :], bank[2 * half + c][:], modc[:, b, 1, c, 0:1],
                                              modc[:, b, 1, c, 1:2], ALU.mult, ALU.add).then_inc(h2_done, 1)
                dve.wait_ge(lg_full, 2 * B + 2)
                logits = bank[lg_bank][:, 0:NT * E].rearrange("p (j e) -> p j e", j=NT)
                link(dve.tensor_reduce(out=lmax[:], in_=logits, axis=AX.X, op=ALU.max))
                dve.tensor_tensor(out=lg[:], in0=logits, in1=lmax[:].unsqueeze(2).to_broadcast([P, NT, E]),
                                  op=ALU.subtract).then_inc(lg_ready, 1)
                dve.wait_ge(lg_exp, 1)
                settled(dve)
                for j in range(NT):
                    ins = dve.max(top[:, j, :], lg[:, j, :])
                link(ins)
                settled(dve)
                for j in range(NT):
                    ins = dve.max_index(top_i[:, j, :], top[:, j, :], lg[:, j, :])
                link(ins)
                dve.wait_ge(consts3, 1)
                link(dve.tensor_copy(top_f[:], top_i[:]))
                for r in range(TOPK):
                    ins = dve.tensor_tensor(out=hit[:, :, r, :], in0=iota16[:].unsqueeze(1).to_broadcast([P, NT, E]),
                                            in1=top_f[:, :, r:r + 1].to_broadcast([P, NT, E]), op=ALU.is_equal)
                link(ins)
                link(dve.tensor_reduce(out=cw[:], in_=hit[:].rearrange("p j r e -> p j e r"), axis=AX.X, op=ALU.add))
                link(dve.tensor_tensor(out=cw[:], in0=cw[:], in1=lg[:], op=ALU.mult))
                link(dve.tensor_reduce(out=wsum[:], in_=cw[:], axis=AX.X, op=ALU.add))
                link(dve.reciprocal(wsum[:], wsum[:]))
                link(dve.tensor_scalar(wsum[:], wsum[:], float(TOPK), None, ALU.mult))
                link(dve.tensor_tensor(out=cw[:], in0=cw[:], in1=wsum[:].unsqueeze(2).to_broadcast([P, NT, E]), op=ALU.mult))
                link(dve.tensor_copy(cw_parts[:, :, 0, :], cw[:]))
                link(dve.tensor_tensor(out=cw_rest[:], in0=cw[:], in1=cw_parts[:, :, 0, :], op=ALU.subtract))
                link(dve.tensor_copy(cw_parts[:, :, 1, :], cw_rest[:]))
                dve.tensor_tensor(out=cw_parts[:, :, 2, :], in0=cw_rest[:], in1=cw_parts[:, :, 1, :],
                                  op=ALU.subtract).then_inc(cwp_done, 1)
        post.close()

        wl_hi = sb(moe, "wl_hi", [P, NLATE, WCOLS], F32R)
        wl_lo = sb(moe, "wl_lo", [P, NLATE, WCOLS], F32R)
        wl_raw = sb(moe, "wl_raw", [P, WCOLS], F32)
        mid = sb(moe, "mid", [P, 2, TT], F32)
        g_hi = sb(moe, "g_hi", [P, 2, TT], F32R)
        g_lo = sb(moe, "g_lo", [P, 2, TT], F32R)
        wl_in, wl_hi_s, wl_lo_s = sem("late_w_loaded"), sem("late_w_high"), sem("late_w_low")
        up_full, silu_done, mult_done, cw_full, cw_used = sem("up_full"), sem("silu_done"), sem("mult_done"), sem("cw_full"), sem("cw_used")
        ghi_done, glo_done, down_done = sem("g_high_done"), sem("g_low_done"), sem("down_done")
        y_read, fin_done, o_out, d4 = sem("y_read"), sem("out_ready"), sem("out_written"), sem("dve_chain4")

        def weights(e):
            return (w_hi[:, e, :], w_lo[:, e, :]) if e < NEARLY else (wl_hi[:, e - NEARLY, :], wl_lo[:, e - NEARLY, :])

        with nc.Block() as block:
            @block.sync
            def _(sp):
                for k in range(NLATE):
                    e = NEARLY + k
                    if k:
                        sp.wait_ge(wl_lo_s, k)
                    if e < E:
                        load_expert(sp, wl_raw[:], we1_in[e], we3_in[e], we2_in[e], wl_in)
                    else:
                        cols = slice((e - E) * H, (e - E + 1) * H)
                        load_expert(sp, wl_raw[:], ws1_in[:, cols], ws3_in[:, cols], ws2_in[cols, :], wl_in)
                with sp.Fori(0, B * T // TT) as t:
                    sp.wait_ge(fin_done, t + 2)
                    sp.dma_start(out_view[:, bass.ds(t * TJ, TJ), :], x_sb[:, bass.ds(t * TJ, TJ), :]).then_inc(o_out, 16)
                sp.wait_ge(o_out, 16 * (B * T // TT))

            @block.gpsimd
            def _(pool):
                for k in range(NLATE):
                    pool.wait_ge(wl_in, 48 * (k + 1))
                    pool.tensor_copy(wl_hi[:, k, :], wl_raw[:]).then_inc(wl_hi_s, 1)
                    pool.wait_ge(wl_hi_s, k + 1)
                    pool.tensor_tensor(out=wl_lo[:, k, :], in0=wl_raw[:], in1=wl_hi[:, k, :].bitcast(F32),
                                       op=ALU.subtract).then_inc(wl_lo_s, 1)

            @block.scalar
            def _(act):
                with act.Fori(0, B * T // TT) as t:
                    def high(e):
                        if e < E:
                            act.wait_ge(cw_used, E * t + e + 1 + 2)
                        else:
                            act.wait_ge(mult_done, NE * t + e + 1 + 2)
                        act.wait_ge(down_done, NE * t + e - 1 + 2)
                        act.activation(g_hi[:, e % 2, :], mid[:, e % 2, :], ACT.Copy).then_inc(ghi_done, 1)
                    for e in range(NE):
                        act.wait_ge(up_full, NE * t + e + 1)
                        act.wait_ge(glo_done, NE * t + e - 1 + 2)
                        if e == 0:
                            act.wait_ge(fin_done, t + 1)
                        act.activation(mid[:, e % 2, :], bank[e % 2][:], ACT.Silu).then_inc(silu_done, 1)
                        if e:
                            high(e - 1)
                    high(NE - 1)

            @block.tensor
            def _(pe):
                pe.sem_inc(down_done, 2)
                with pe.Fori(0, B * T // TT) as t:
                    at = t * TT

                    def up(e):
                        hi, lo = weights(e)
                        if e >= NEARLY:
                            pe.wait_ge(wl_lo_s, e - NEARLY + 1)
                        pe.wait_ge(silu_done, NE * t + e - 1 + 2)
                        pe.wait_ge(mult_done, NE * t + e - 1 + 2)
                        for m in range(2):
                            n = 0
                            for w, h in ((hi, h2_hi), (lo, h2_hi), (hi, h2_lo)):
                                for c in range(DC):
                                    col = c * 2 * H + m * H
                                    last = pe.matmul(bank[2 * m + e % 2][:], w[:, col:col + H], h[:, c, bass.ds(at, TT)],
                                                     start=(n == 0), stop=(n == 5))
                                    n += 1
                        last.then_inc(up_full, 1)
                        if e < E:
                            pe.wait_ge(cw_used, E * t + e - 1 + 2)
                            settled(pe)
                            pe.matmul(bank[4 + e % 2][:], sel[:, e, :], cw_t[:, bass.ds(at, TT)], start=True, stop=True)\
                              .then_inc(cw_full, 1)

                    def down(e):
                        hi, lo = weights(e)
                        pe.wait_ge(glo_done, NE * t + e + 1 + 2)
                        if e == 0:
                            pe.wait_ge(y_read, t + 1)
                        for g, w in ((g_hi, hi), (g_lo, hi), (g_hi, lo)):
                            for j in range(TJ):
                                first = e == 0 and g is g_hi and w is hi and j % 2 == 0
                                last = pe.matmul(bank[6 + j // 2][:, (j % 2) * D:(j % 2 + 1) * D],
                                                 g[:, e % 2, j * P:(j + 1) * P], w[:, W13:WCOLS],
                                                 start=first, stop=(e == NE - 1 and w is lo), skip_group_check=True)
                        last.then_inc(down_done, 1)

                    for e in range(NE):
                        up(e)
                        if e >= 2:
                            down(e - 2)
                    down(NE - 2)
                    down(NE - 1)

            @block.vector
            def _(dve):
                for s_, n in ((glo_done, 2), (silu_done, 2), (mult_done, 2), (cw_used, 2), (y_read, 1), (fin_done, 1)):
                    dve.sem_inc(s_, n)
                with dve.Fori(0, B) as b, dve.Fori(0, 2) as half:
                    t = 2 * b + half

                    def low(e):
                        dve.wait_ge(ghi_done, NE * t + e + 1)
                        dve.tensor_tensor(out=g_lo[:, e % 2, :], in0=mid[:, e % 2, :], in1=g_hi[:, e % 2, :].bitcast(F32),
                                          op=ALU.subtract).then_inc(glo_done, 1)
                    for e in range(NE):
                        m = mid[:, e % 2, :]
                        dve.wait_ge(silu_done, NE * t + e + 1 + 2)
                        ins = dve.tensor_tensor(out=m, in0=m, in1=bank[2 + e % 2][:], op=ALU.mult)
                        ins.then_inc(mult_done, 1)
                        if e < E:
                            dve.wait_ge(mult_done, NE * t + e + 1 + 2)
                            dve.wait_ge(cw_full, E * t + e + 1)
                            dve.tensor_tensor(out=m, in0=m, in1=bank[4 + e % 2][:], op=ALU.mult).then_inc(cw_used, 1)
                        if e:
                            low(e - 1)
                    low(NE - 1)
                    dve.wait_ge(down_done, NE * (t + 1) + 2)
                    sums = psum[:, 6:8, :].rearrange("p a (c d) -> p (a c) d", c=2)
                    out_tile = x_sb[:, bass.ds(t * TJ, TJ), :]
                    fin = mid[:].rearrange("p a (c d) -> p (a c) d", c=2)
                    ins = dve.tensor_tensor(out=fin, in0=sums, in1=gate[:, 1, bass.ds(b, 1), :].to_broadcast([P, TJ, D]), op=ALU.mult)
                    ins.then_inc(y_read, 1)
                    dve.wait_ge(y_read, t + 2)
                    dve.tensor_tensor(out=out_tile, in0=out_tile, in1=fin, op=ALU.add).then_inc(fin_done, 1)
        moe.close()


_INS = ["L0_attn_x", "L0_attn_wq", "L0_attn_wk", "L0_attn_wv", "L0_attn_wo", "L0_ffn_w_router", "L0_ffn_we1",
        "L0_ffn_we3", "L0_ffn_we2", "L0_ffn_ws1", "L0_ffn_ws3", "L0_ffn_ws2", "L0_c", "L0_wmod"]


def kernel(**inputs):
    import numpy as _np
    import concourse.bacc as _bacc
    from concourse import mybir as _mybir
    from concourse.bass_utils import run_bass_kernel_spmd as _run

    nc = _bacc.Bacc("TRN2", target_bir_lowering=False, num_devices=1)
    arrays, args = {}, []
    for name in _INS:
        a = _np.ascontiguousarray(inputs[name])
        arrays[f"in_{name}_dram"] = a
        args.append(nc.dram_tensor(f"in_{name}_dram", a.shape, _mybir.dt.from_np(a.dtype), kind="ExternalInput").ap())
    args.append(nc.dram_tensor("out_0_dram", (B, T, D), _mybir.dt.float32, kind="ExternalOutput").ap())
    block_kernel(nc, *args)
    r = _run(nc, [arrays], core_ids=[0])
    return r.results[0]["out_0_dram"]
```

```python
from contextlib import ExitStack

import concourse.bass as bass
from concourse import mybir

F32 = mybir.dt.float32
F32R = mybir.dt.float32r
U32 = mybir.dt.uint32
ALU = mybir.AluOpType
ACT = mybir.ActivationFunctionType
AX = mybir.AxisListType

P = 128
B, T, D = 2, 1024, 256
NH, NKV, HD = 32, 8, 8
REP = NH // NKV
DC = D // P
TT = 512
TJ = TT // P
NT = B * T // P
NPASS = B * T // TT
GROUPS = B * NKV
TC = T // P
E, H, HS, TOPK = 16, 128, 512, 4
NE = E + HS // H
NEARLY = 4
NLATE = NE - NEARLY
WCOLS = DC * 2 * H + D
W13 = DC * 2 * H
EPS = 1e-5
SCALE = HD ** -0.5
LEAST = -3.0e38
MASKED = -1.0e30
PROD = 4 * HD
STACK = PROD + 2

STEPS = [(0, c, c * P) for c in range(TC // 2)] + [(1, c, max(0, c - TC // 2) * P) for c in range(TC)]
NSTEP = len(STEPS)


def max_units():
    units = []
    for i in range(TC):
        n, key, part = i + 1, 0, 0
        while n >= 4:
            units += [(i, h, 1, key, 4 * P, part) for h in range(REP)]
            n, key, part = n - 4, key + 4 * P, part + 1
        if n >= 2:
            units += [(i, h, 2, key, 2 * P, part) for h in (0, 2)]
            n, key, part = n - 2, key + 2 * P, part + 1
        if n:
            units += [(i, 0, 4, key, P, part)]
    return units


UNITS = max_units()
NU = len(UNITS)
PARTS = 1 + max(u[5] for u in UNITS)
NB = 3
WITH = [4, 3, 2, 1, 4, 4, 4, 4, 4, 2, 2, 2]
AHEAD = sum(WITH[9:])
TURN = 10
LAG = 2
assert sum(WITH) == NU and NU % NB == 0 and NSTEP % (LAG + 1) == 0


class Chain:

    def __init__(self, eng, sem, start):
        self.eng, self.sem, self.count, self.start = eng, sem, 0, start

    def link(self, ins):
        self.count += 1
        ins.then_inc(self.sem, 1)
        self.eng.wait_ge(self.sem, self.start + self.count)


def block_kernel(nc, x_in, wq_in, wk_in, wv_in, wo_in, wr_in, we1_in, we3_in, we2_in,
                 ws1_in, ws3_in, ws2_in, c_in, wmod_in, out):
    q_dram = nc.dram_tensor("q_parts", (GROUPS, 2 * HD, REP, T), F32, kind="Internal").ap()
    k_dram = nc.dram_tensor("k_parts", (2, GROUPS * HD, T), F32, kind="Internal").ap()
    y_dram = nc.dram_tensor("y_sums", (GROUPS, P, T), F32, kind="Internal").ap()
    r_dram = nc.dram_tensor("row_reciprocals", (B, NH, T), F32, kind="Internal").ap()

    x_view = x_in.rearrange("b (n p) d -> p (b n) d", p=P)
    out_view = out.rearrange("b (n p) d -> p (b n) d", p=P)

    whole = ExitStack()
    with whole:
        def sb(stack, name, shape, dt):
            return stack.enter_context(nc.sbuf_tensor(name, shape, dt))

        def sem(name):
            return whole.enter_context(nc.semaphore(name))

        psum = whole.enter_context(nc.psum_tensor("psum", [P, 8, 512], F32))
        bank = [psum[:, i, :] for i in range(8)]

        x_sb = sb(whole, "x_sb", [P, NT, D], F32)
        w_hi = sb(whole, "w_hi", [P, NEARLY, WCOLS], F32R)
        w_lo = sb(whole, "w_lo", [P, NEARLY, WCOLS], F32R)
        gate = sb(whole, "gate", [P, 2, B, D], F32)
        modc = sb(whole, "modc", [P, B, 2, DC, 2], F32)
        ident = sb(whole, "ident", [P, P], F32)
        wo_sb = sb(whole, "wo_sb", [P, DC, D], F32)
        wr_sb = sb(whole, "wr_sb", [P, DC, E], F32)
        stats = sb(whole, "stats", [P, NT, 6], F32)
        mv = sb(whole, "mv", [P, NT, 2], F32)
        sd = sb(whole, "sd", [P, NT], F32)
        rstd = sb(whole, "rstd", [P, NT], F32)

        def settled(eng):
            eng.sem_inc(passed, 1)

        passed = sem("passed")

        def moments(dve, link, tile):
            settled(dve)
            for j in range(TJ):
                ins = dve.bn_stats(stats[:, tile + j, :], x_sb[:, tile + j, :])
            link(ins)

        def deviations(dve, link, b, sqrt_ready, sqrt_done):
            tiles = slice(b * TC, (b + 1) * TC)
            settled(dve)
            for j in range(b * TC, (b + 1) * TC):
                ins = dve.bn_aggr(mv[:, j, :], stats[:, j, :])
            link(ins)
            dve.tensor_scalar(sd[:, tiles], mv[:, tiles, 1], EPS, None, ALU.add).then_inc(sqrt_ready, 1)
            dve.wait_ge(sqrt_done, b + 1)
            link(dve.reciprocal(rstd[:, tiles], sd[:, tiles]))

        def square_roots(act, b, ready, done):
            tiles = slice(b * TC, (b + 1) * TC)
            act.wait_ge(ready, b + 1)
            act.activation(sd[:, tiles], sd[:, tiles], ACT.Sqrt).then_inc(done, 1)

        def normalise(dve, tile, xn):
            for j in range(TJ):
                ins = dve.tensor_scalar(xn[:, j, :], x_sb[:, tile + j, :], mv[:, tile + j, 0:1],
                                        rstd[:, bass.ds(tile + j, 1)], ALU.subtract, ALU.mult)
            return ins

        attn = ExitStack()
        qa, qb = [[sb(attn, f"{n}{k}", [P, REP, T], F32R) for k in range(2)] for n in ("qa", "qb")]
        ka, kb = [[sb(attn, f"{n}{k}", [P, T], F32R) for k in range(2)] for n in ("ka", "kb")]
        v_all = sb(attn, "v_all", [P, GROUPS, TC, HD], F32)
        k_parts = sb(attn, "k_parts_sb", [NKV * HD, 2, 2, TT], F32)
        v_aug = sb(attn, "v_aug", [P, 2, TC, 32], F32)
        causal = sb(attn, "causal", [P, TT], F32)
        l_sb = sb(attn, "l_sb", [P, T // 4], F32)

        consts2 = sem("consts2_ready")
        qa_in, qb_in = [[sem(f"{n}_{k}") for k in range(2)] for n in ("qa_loaded", "qb_loaded")]

        def load_stacks(eng, group, q_tile, k_tile, par, loaded):
            for part in range(2):
                rows = slice(part * 2 * HD, (part + 1) * 2 * HD)
                eng.dma_start(q_tile[par][rows].bitcast(F32), q_dram[group]).then_inc(loaded[par], 16)
                k_rows = k_dram[part, bass.ds(group * HD, HD), :].unsqueeze(0).to_broadcast([2, HD, T])
                eng.dma_start(k_tile[par][rows, :].bitcast(F32), k_rows).then_inc(loaded[par], 16)

        pro = ExitStack()
        wq_sb = sb(pro, "wq_sb", [P, DC, NH * HD], F32)
        wk_sb = sb(pro, "wk_sb", [P, DC, NKV * HD], F32)
        wv_sb = sb(pro, "wv_sb", [P, DC, NKV * HD], F32)
        wmod_sb = sb(pro, "wmod_sb", [P, DC, 6 * D], F32)
        c_sb = sb(pro, "c_sb", [P, DC, B], F32)
        c_rep = sb(pro, "c_rep", [P, DC, B, P], F32)
        g_rows = sb(pro, "g_rows", [P, 2, B, D], F32)
        g_sign = sb(pro, "g_sign", [P, 2, B, D], F32)
        g_size = sb(pro, "g_size", [P, 2, B, D], F32)
        xn = sb(pro, "xn", [P, 2, TJ, D], F32)
        h_t = sb(pro, "h_t", [P, 2, DC, TT], F32)
        q_parts = [w[:].rearrange("p e n -> p (e n)")[:, 0:2 * DC * TT].rearrange("p (a m t) -> p a m t", a=2, m=DC)
                   for w in (w_hi, w_lo)]

        c_in_s, wmod_s, wmod_g_s, wqkv_s, wor_s = sem("c_loaded"), sem("wmod_loaded"), sem("wmod_gates_loaded"), sem("wqkv_loaded"), sem("wo_wr_loaded")
        x_s = [sem(f"x_loaded_{k}") for k in range(2 * B)]
        gates_read, p1 = sem("gates_read"), sem("pool_chain1")
        consts_s, c_silu, c_repd = sem("consts_ready"), sem("c_silu"), sem("c_repeated")
        modc_mm, gate_mm, mod_done = sem("modc_mm"), sem("gate_mm"), sem("mod_done")
        d1 = sem("dve_chain1")
        var1, sqrt1, xn1 = sem("var1_ready"), sem("sqrt1_done"), sem("xn1_ready")
        xt_full, ht_ready = sem("xt_full"), sem("ht_ready")
        q_full, k_full, v_full = sem("q_full"), sem("k_full"), sem("v_full")
        hi_done, lo_done, v_done = sem("qk_high_done"), sem("qk_low_done"), sem("v_done")
        qk_out = [sem(f"qk_out_{k}") for k in range(2)]
        OUTS1 = 16 * (2 * DC + 2)
        zeros_s = sem("stacks_zeroed")
        MODCOLS = [1, 0, 4, 3]
        GATES = (2, 5)
        wmod_view = wmod_in.rearrange("(c p) n -> p c n", p=P)
        QKV = DC + 1

        with nc.Block() as block:
            @block.sync
            def _(sp):
                sp.dma_start(c_sb[:, :, 0], c_in[0, :].rearrange("(c p) -> p c", p=P),
                             allow_slow_non_contiguous=True).then_inc(c_in_s, 16)
                sp.dma_start(c_sb[:, :, 1], c_in[1, :].rearrange("(c p) -> p c", p=P),
                             allow_slow_non_contiguous=True).then_inc(c_in_s, 16)
                for g, which in enumerate(GATES):
                    sp.dma_start(wmod_sb[:, :, which * D:(which + 1) * D],
                                 wmod_view[:, :, which * D:(which + 1) * D]).then_inc(wmod_g_s, 16)
                for q in range(4):
                    sp.dma_start(x_sb[:, q * TJ:(q + 1) * TJ, :], x_view[:, q * TJ:(q + 1) * TJ, :]).then_inc(x_s[q], 16)
                for which in MODCOLS:
                    sp.dma_start(wmod_sb[:, :, which * D:(which + 1) * D],
                                 wmod_view[:, :, which * D:(which + 1) * D]).then_inc(wmod_s, 16)
                sp.dma_start(wq_sb[:], wq_in.rearrange("(c p) n -> p c n", p=P)).then_inc(wqkv_s, 16)
                sp.dma_start(wk_sb[:], wk_in.rearrange("(c p) n -> p c n", p=P)).then_inc(wqkv_s, 16)
                sp.dma_start(wv_sb[:], wv_in.rearrange("(c p) n -> p c n", p=P)).then_inc(wqkv_s, 16)
                sp.dma_start(wo_sb[:], wo_in.rearrange("(c p) n -> p c n", p=P)).then_inc(wor_s, 16)
                sp.dma_start(wr_sb[:], wr_in.rearrange("(c p) n -> p c n", p=P)).then_inc(wor_s, 16)
                for b in range(B):
                    for half in range(2):
                        n = 2 * b + half + 1
                        toks = slice(half * TT, (half + 1) * TT)
                        for m in range(DC):
                            sp.wait_ge(lo_done, QKV * n + m + 1)
                            for part in range(2):
                                sp.dma_start(q_dram[b * NKV + 4 * m:b * NKV + 4 * m + 4, part * HD:(part + 1) * HD, :, toks],
                                             q_parts[half][:, part, m, :].bitcast(F32)).then_inc(qk_out[half], 16)
                        sp.wait_ge(lo_done, QKV * n + QKV)
                        for part in range(2):
                            sp.dma_start(k_dram[part, b * NKV * HD:(b + 1) * NKV * HD, toks],
                                         k_parts[:, half, part, :]).then_inc(qk_out[half], 16)
                    if b == 0:
                        sp.wait_ge(zeros_s, 6)
                        for half in range(2):
                            sp.wait_ge(qk_out[half], 16 + OUTS1)
                        load_stacks(sp, 0, qa, ka, 0, qa_in)
                        load_stacks(sp, 0, qb, kb, 0, qb_in)
                        load_stacks(sp, 1, qa, ka, 1, qa_in)
                sp.wait_ge(wor_s, 32)

            @block.gpsimd
            def _(pool):
                pool.memset(ident[:], 0.0).then_inc(consts_s, 1)
                pool.wait_ge(consts_s, 1)
                pool.affine_select(out=ident[:, :], in_=ident[:, :], compare_op=ALU.not_equal, fill=1.0, base=0,
                                   pattern=[[-1, P]], channel_multiplier=1).then_inc(consts_s, 1)
                stacks = (ka[0], kb[0], ka[1], qa[0], qb[0], qa[1], kb[1], qb[1])
                for tile in stacks[:6]:
                    pool.memset(tile[:].bitcast(F32), 0.0).then_inc(zeros_s, 1)
                chain = Chain(pool, p1, 0)
                pool.wait_ge(gates_read, 1)
                chain.link(pool.tensor_scalar(g_sign[:], g_rows[:], 0.0, 2.0, ALU.is_ge, ALU.mult))
                chain.link(pool.tensor_scalar(g_sign[:], g_sign[:], -1.0, None, ALU.add))
                chain.link(pool.tensor_tensor(out=g_size[:], in0=g_rows[:], in1=g_sign[:], op=ALU.mult))
                chain.link(pool.tensor_scalar(g_size[:], g_size[:], 0.25, None, ALU.max))
                chain.link(pool.tensor_tensor(out=gate[:], in0=g_sign[:], in1=g_size[:], op=ALU.mult))
                pool.tensor_scalar(gate[:, 1, :, :], gate[:, 1, :, :], 1.0 / (TOPK + 1), None, ALU.mult)
                for tile in stacks[6:]:
                    pool.memset(tile[:].bitcast(F32), 0.0).then_inc(zeros_s, 1)
                pool.memset(causal[:], 0.0).then_inc(consts2, 1)
                pool.memset(v_aug[:], 1.0).then_inc(consts2, 1)
                pool.wait_ge(consts2, 2)
                pool.affine_select(out=causal[:, TT - P:TT], in_=causal[:, TT - P:TT], compare_op=ALU.is_ge, fill=MASKED,
                                   base=0, pattern=[[-1, P]], channel_multiplier=1).then_inc(consts2, 1)

            @block.scalar
            def _(act):
                for half in range(2):
                    act.sem_inc(qk_out[half], 16)
                act.wait_ge(c_in_s, 32)
                act.activation(c_sb[:], c_sb[:], ACT.Silu).then_inc(c_silu, 1)
                square_roots(act, 0, var1, sqrt1)
                act.wait_ge(gate_mm, 1)
                act.activation(g_rows[:], psum[:, 6:8, :].rearrange("p g (b d) -> p g b d", b=B), ACT.Copy).then_inc(gates_read, 1)
                square_roots(act, 1, var1, sqrt1)
                with act.Fori(0, B) as b:
                    for half in range(2):
                        n = 2 * b + half + 1
                        act.wait_ge(qk_out[half], OUTS1 * b + 16)
                        for m in range(DC):
                            act.wait_ge(q_full, DC * (n - 1) + m + 1)
                            act.activation(q_parts[half][:, 0, m, :], bank[2 + m][:], ACT.Copy).then_inc(hi_done, 1)
                        act.wait_ge(k_full, n)
                        act.activation(k_parts[:, half, 0, :].bitcast(F32R), bank[4][0:NKV * HD, :], ACT.Copy).then_inc(hi_done, 1)

            @block.tensor
            def _(pe):
                pe.wait_ge(wmod_g_s, 32)
                pe.wait_ge(c_repd, 1)
                for g, which in enumerate(GATES):
                    for b in range(B):
                        for kc in range(DC):
                            last = pe.matmul(bank[6 + g][:, b * D:(b + 1) * D], c_rep[:, kc, b, :],
                                             wmod_sb[:, kc, which * D:(which + 1) * D],
                                             start=(kc == 0), stop=(kc == DC - 1))
                last.then_inc(gate_mm, 1)
                def transposes(n):
                    half = (n - 1) % 2
                    pe.wait_ge(xn1, n)
                    for c in range(DC):
                        for j in range(TJ):
                            last = pe.transpose(bank[6 * half + c][:, j * P:(j + 1) * P],
                                                xn[:, half, j, c * P:(c + 1) * P], ident[:])
                        last.then_inc(xt_full, 1)

                def modulation():
                    pe.wait_ge(wmod_s, 64)
                    for k, which in enumerate(MODCOLS):
                        for c in range(DC):
                            for kc in range(DC):
                                last = pe.matmul(bank[5][:, (k * DC + c) * B:(k * DC + c + 1) * B],
                                                 wmod_sb[:, kc, which * D + c * P:which * D + (c + 1) * P],
                                                 c_sb[:, kc, :], start=(kc == 0), stop=(kc == DC - 1))
                    last.then_inc(modc_mm, 1)

                def projections(n):
                    half = (n - 1) % 2
                    pe.wait_ge(ht_ready, DC * n)
                    for m in range(DC):
                        pe.wait_ge(lo_done, QKV * (n - 1) + m + 1)
                        for kc in range(DC):
                            last = pe.matmul(bank[2 + m][:], wq_sb[:, kc, m * P:(m + 1) * P], h_t[:, half, kc, :],
                                             start=(kc == 0), stop=(kc == DC - 1))
                        last.then_inc(q_full, 1)
                    pe.wait_ge(lo_done, QKV * (n - 1) + QKV)
                    for kc in range(DC):
                        last = pe.matmul(bank[4][0:NKV * HD, :], wk_sb[:, kc, :], h_t[:, half, kc, :],
                                         start=(kc == 0), stop=(kc == DC - 1))
                    last.then_inc(k_full, 1)
                    pe.wait_ge(v_done, n)
                    for j in range(TJ):
                        for kc in range(DC):
                            last = pe.matmul(bank[5][:, j * NKV * HD:(j + 1) * NKV * HD],
                                             h_t[:, half, kc, j * P:(j + 1) * P], wv_sb[:, kc, :],
                                             start=(kc == 0), stop=(kc == DC - 1))
                    last.then_inc(v_full, 1)

                pe.wait_ge(gates_read, 1)
                pe.wait_ge(consts_s, 2)
                transposes(1)
                transposes(2)
                modulation()
                pe.wait_ge(mod_done, 1)
                pe.wait_ge(wqkv_s, 16 * 3)
                for n in range(1, NPASS + 1):
                    projections(n)
                    if n + 2 <= NPASS:
                        transposes(n + 2)

            @block.vector
            def _(dve):
                dve.sem_inc(v_done, 1)
                dve.sem_inc(lo_done, QKV)
                chain = Chain(dve, d1, 0)
                dve.wait_ge(c_silu, 1)
                dve.tensor_copy(c_rep[:], c_sb[:].unsqueeze(3).to_broadcast([P, DC, B, P])).then_inc(c_repd, 1)
                for q in range(2 * B):
                    dve.wait_ge(x_s[q], 16)
                    moments(dve, chain.link, q * TJ)
                    if q == 1:
                        deviations(dve, chain.link, 0, var1, sqrt1)
                        for n in (1, 2):
                            normalise(dve, (n - 1) * TJ, xn[:, n - 1]).then_inc(xn1, 1)

                def shifted(n):
                    b, half = (n - 1) // 2, (n - 1) % 2
                    for c in range(DC):
                        dve.wait_ge(xt_full, DC * (n - 1) + c + 1)
                        dve.tensor_scalar(h_t[:, half, c, :], bank[6 * half + c][:], modc[:, b, 0, c, 0:1],
                                          modc[:, b, 0, c, 1:2], ALU.mult, ALU.add).then_inc(ht_ready, 1)

                def parts(n):
                    b, half = (n - 1) // 2, (n - 1) % 2
                    for m in range(DC):
                        dve.wait_ge(hi_done, QKV * (n - 1) + m + 1)
                        dve.tensor_tensor(out=q_parts[half][:, 1, m, :], in0=bank[2 + m][:],
                                          in1=q_parts[half][:, 0, m, :].bitcast(F32), op=ALU.subtract).then_inc(lo_done, 1)
                    dve.wait_ge(hi_done, QKV * n)
                    dve.tensor_tensor(out=k_parts[:, half, 1, :].bitcast(F32R), in0=bank[4][0:NKV * HD, :],
                                      in1=k_parts[:, half, 0, :], op=ALU.subtract).then_inc(lo_done, 1)
                    dve.wait_ge(v_full, n)
                    dve.tensor_copy(v_all[:, b * NKV:(b + 1) * NKV, half * TJ:(half + 1) * TJ, :]
                                    .rearrange("p g j d -> p j g d"),
                                    bank[5][:, 0:TJ * NKV * HD].rearrange("p (j g d) -> p j g d", j=TJ, g=NKV))\
                       .then_inc(v_done, 1)

                dve.wait_ge(modc_mm, 1)
                for norm in range(2):
                    cols = bank[5][:, 8 * norm:8 * norm + 8].rearrange("p (k c b) -> p b c k", k=2, c=DC)
                    ins = dve.tensor_copy(modc[:, :, norm, :, :], cols)
                chain.link(ins)
                dve.tensor_scalar(modc[:, :, :, :, 0], modc[:, :, :, :, 0], 1.0, None, ALU.add).then_inc(mod_done, 1)
                dve.wait_ge(mod_done, 1)
                shifted(1)
                shifted(2)
                deviations(dve, chain.link, 1, var1, sqrt1)
                for n in range(1, NPASS + 1):
                    if n + 2 <= NPASS:
                        normalise(dve, (n + 1) * TJ, xn[:, (n - 1) % 2]).then_inc(xn1, 1)
                    parts(n)
                    if n + 2 <= NPASS:
                        shifted(n + 2)
        pro.close()

        core = ExitStack()
        probs = sb(core, "probs", [P, LAG + 1, REP, TT], F32)
        y_sb = sb(core, "y_sb", [P, 2, TT], F32)
        max_parts = sb(core, "max_parts", [P, REP, TC, PARTS], F32)
        neg_max = sb(core, "neg_max", [P, 2, REP * TC], F32)
        neg_max_f = sb(core, "neg_max_f", [P, REP * TC], F32)
        neg_max_t = sb(core, "neg_max_t", [2 * REP * TC, P], F32)
        w_raw = sb(core, "w_raw", [P, 2, WCOLS], F32)

        unit_bank, sum_bank = (4, 5, 6), 7
        raw_in = [sem(f"raw_loaded_{k}") for k in range(2)]
        row_in, y_out = [[sem(f"{n}_{k}") for k in range(2)] for n in ("max_rows_loaded", "sums_out")]
        v_aug_s, parts_set = sem("v_aug_ready"), sem("max_parts_set")
        unit_full, unit_free = sem("unit_full"), sem("unit_free")
        negm_done, negt_full, negt_done = sem("neg_max_done"), sem("neg_max_t_full"), sem("neg_max_t_done")
        st_full, p_full, p_masked, pv_done = sem("scores_full"), sem("probs_full"), sem("probs_masked"), sem("pv_done")
        y_done, hi2, lo2, d2 = sem("sums_copied"), sem("w_high_done"), sem("w_low_done"), sem("dve_chain2")
        LOADS = 16 * 4
        NDIAG = TC

        l_in = [sem(f"l_loaded_{b}") for b in range(B)]
        l_recip, r_out = sem("l_reciprocal"), [sem(f"r_out_{b}") for b in range(B)]

        def row_sums_in(eng, b, tile, loaded):
            rows = y_dram[b * NKV:(b + 1) * NKV].rearrange("g (h r) (q t) -> g h r q t", r=32, q=4)
            eng.dma_start(tile[:], rows[:, :, HD, :, :]).then_inc(loaded, 16)

        def reciprocals_out(eng, b, tile):
            eng.dma_start(r_dram[b].rearrange("n (q t) -> (n q) t", q=4), tile[:]).then_inc(r_out[b], 16)

        def wait_if(eng, s, value):
            if not isinstance(value, int) or value > 0:
                eng.wait_ge(s, value)

        def load_expert(eng, raw, w1, w3, w2, loaded):
            cols = raw[:, 0:W13].rearrange("p (c w h) -> p c w h", c=DC, w=2)
            eng.dma_start(cols[:, :, 0, :], w1.rearrange("(c p) h -> p c h", p=P)).then_inc(loaded, 16)
            eng.dma_start(cols[:, :, 1, :], w3.rearrange("(c p) h -> p c h", p=P)).then_inc(loaded, 16)
            eng.dma_start(raw[:, W13:WCOLS], w2).then_inc(loaded, 16)

        def periods(eng, period):
            period(0, 0)
            period(0, 1)
            with eng.Fori(1, NEARLY // 2) as it:
                period(it, 0)
                period(it, 1)
            with eng.Fori(NEARLY // 2, GROUPS // 2 - 1) as it:
                period(it, 0, weights=False)
                period(it, 1, weights=False)
            period(GROUPS // 2 - 1, 0, last=1)
            period(GROUPS // 2 - 1, 1, last=2)

        def ahead(it, par, s, last):
            for u in range(sum(WITH[:s]) + AHEAD, sum(WITH[:s + 1]) + AHEAD):
                if u < NU and last < 2:
                    yield (it + par, 1 - par, u)
                elif u >= NU and last < 1:
                    yield (it + 1, par, u - NU)

        with nc.Block() as block:
            @block.sync
            def _(sp):
                def rows_in(it, par):
                    sp.wait_ge(negt_done, 2 * it + par + 1)
                    for part in range(2):
                        row = PROD + part
                        sp.dma_start(qb[par][row:row + 1].bitcast(F32),
                                     neg_max_t[part * REP * TC:(part + 1) * REP * TC, :]).then_inc(row_in[par], 16)

                def sums_out(group, half):
                    sp.wait_ge(y_done, 2 * group + half + 1)
                    sp.dma_start(y_dram[group, :, half * TT:(half + 1) * TT], y_sb[:, half, :]).then_inc(y_out[half], 16)

                def period(it, par, last=0, weights=True):
                    group = 2 * it + par
                    if last < 2:
                        wait_if(sp, st_full, 2 * NSTEP * group)
                        load_stacks(sp, group + 1, qb, kb, 1 - par, qb_in)
                    if last < 1:
                        sp.wait_ge(unit_full, NU * (group + 1))
                        load_stacks(sp, group + 2, qa, ka, par, qa_in)
                    if weights and last < 1:
                        wait_if(sp, lo2, group - 1)
                        load_expert(sp, w_raw[:, par, :], we1_in[group], we3_in[group], we2_in[group], raw_in[par])
                    if not (isinstance(group, int) and group == 0):
                        sums_out(group - 1, 1)
                    sums_out(group, 0)
                    if last < 2:
                        rows_in(it + par, 1 - par)

                rows_in(0, 0)
                for half in range(2):
                    sp.wait_ge(qk_out[half], 16 + OUTS1 * B)
                periods(sp, period)
                for k in range(2):
                    sp.wait_ge(y_out[k], 16 * (GROUPS - 1))
                row_sums_in(sp, 0, l_sb, l_in[0])
                sp.wait_ge(l_recip, 1)
                reciprocals_out(sp, 0, l_sb)
                sums_out(GROUPS - 1, 1)
                for k in range(2):
                    sp.wait_ge(y_out[k], 16 * GROUPS)
                sp.wait_ge(r_out[0], 16)

            @block.gpsimd
            def _(pool):
                def values(group, par):
                    pool.tensor_copy(v_aug[:, par, :, 0:HD], v_all[:, group, :, :]).then_inc(v_aug_s, 1)

                def period(it, par, last=0, weights=True):
                    group = 2 * it + par
                    for s, (half, c, off) in enumerate(STEPS):
                        if c >= half * (TC // 2):
                            pool.wait_ge(p_full, 2 * NSTEP * group + 2 * s + 2)
                            tile = probs[:, s % (LAG + 1), :, off:off + P]
                            settled(pool)
                            pool.affine_select(out=tile, in_=tile, compare_op=ALU.is_ge, fill=0.0, base=0,
                                               pattern=[[0, REP], [1, P]], channel_multiplier=-1).then_inc(p_masked, 1)
                        if s == 3 and last < 2:
                            wait_if(pool, pv_done, NSTEP * group)
                            values(group + 1, 1 - par)
                        if s == 4 and weights and last < 1:
                            pool.wait_ge(hi2, group + 1)
                            pool.tensor_tensor(out=w_lo[:, group, :], in0=w_raw[:, par, :],
                                               in1=w_hi[:, group, :].bitcast(F32), op=ALU.subtract).then_inc(lo2, 1)

                values(0, 0)
                periods(pool, period)

            @block.scalar
            def _(act):
                def turned(it, par):
                    group = 2 * it + par
                    act.wait_ge(negt_full, group + 1)
                    wait_if(act, row_in[1 - par], 32 * (it + par))
                    act.activation(neg_max_t[:], bank[unit_bank[0]][0:2 * REP * TC, 0:P], ACT.Copy).then_inc(negt_done, 1)

                def sums(group, half):
                    act.wait_ge(pv_done, NSTEP * group + (TC // 2, NSTEP)[half])
                    wait_if(act, y_out[half], 16 * group)
                    act.activation(y_sb[:, half, :], bank[sum_bank][:, :], ACT.Copy).then_inc(y_done, 1)

                def period(it, par, last=0, weights=True):
                    group = 2 * it + par
                    for s, (half, c, off) in enumerate(STEPS):
                        wait_if(act, pv_done, NSTEP * group + s - LAG)
                        for pair in range(2):
                            act.wait_ge(st_full, 2 * NSTEP * group + 2 * s + pair + 1)
                            act.activation(probs[:, s % (LAG + 1), 2 * pair:2 * pair + 2, off:TT],
                                           psum[:, 2 * pair:2 * pair + 2, off:TT], ACT.Exp, scale=SCALE).then_inc(p_full, 1)
                        if s == 1 and not (isinstance(group, int) and group == 0):
                            sums(group - 1, 1)
                        if s == 5:
                            sums(group, 0)
                        if s == 3 and weights and last < 1:
                            act.wait_ge(raw_in[par], 48 * (it + 1))
                            act.activation(w_hi[:, group, :], w_raw[:, par, :], ACT.Copy).then_inc(hi2, 1)
                        if s == 9 and last < 2:
                            turned(it + par, 1 - par)

                turned(0, 0)
                periods(act, period)
                sums(GROUPS - 1, 1)

            @block.tensor
            def _(pe):
                def unit(it, par, u):
                    i, h0, nh, key, w, _ = UNITS[u]
                    group, bk = 2 * it + par, bank[unit_bank[u % NB]]
                    if u == 0:
                        pe.wait_ge(qa_in[par], LOADS * (it + 1))
                    wait_if(pe, unit_free, NU * group + u - NB + 1)
                    if u == NB:
                        wait_if(pe, negt_done, group)
                    for k in range(nh):
                        last = pe.matmul(bk[:, k * w:(k + 1) * w], qa[par][:, h0 + k, i * P:(i + 1) * P],
                                         ka[par][:, key:key + w], start=(k == 0),
                                         stop=(k == nh - 1), skip_group_check=True)
                    last.then_inc(unit_full, 1)

                def turn(it, par, followed):
                    group = 2 * it + par
                    pe.wait_ge(negm_done, group + 1)
                    pe.wait_ge(unit_free, NU * (group + 1) + followed)
                    settled(pe)
                    pe.transpose(bank[unit_bank[0]][0:2 * REP * TC, 0:P],
                                 neg_max[:].rearrange("p a n -> p (a n)"), ident[:]).then_inc(negt_full, 1)

                def scores(it, par, s, pair):
                    half, c, off = STEPS[s]
                    group = 2 * it + par
                    if s == 0 and pair == 0:
                        pe.wait_ge(qb_in[par], LOADS * (it + 1))
                        pe.wait_ge(row_in[par], 32 * (it + 1))
                    wait_if(pe, p_full, 2 * NSTEP * group + 2 * s + pair - 1)
                    for h in (2 * pair, 2 * pair + 1):
                        last = pe.matmul(bank[h][:, off:TT], kb[par][:, c * P:(c + 1) * P],
                                         qb[par][:, h, half * TT + off:(half + 1) * TT],
                                         start=True, stop=True)
                    last.then_inc(st_full, 1)

                def product(it, par, s):
                    half, c, off = STEPS[s]
                    group = 2 * it + par
                    if s == 0:
                        pe.wait_ge(v_aug_s, group + 1)
                    if c == 0:
                        wait_if(pe, y_done, 2 * group + half)
                    pe.wait_ge(p_full, 2 * NSTEP * group + 2 * s + 2)
                    if c >= half * (TC // 2):
                        pe.wait_ge(p_masked, NDIAG * group + c + 1)
                    for h in range(REP):
                        last = pe.matmul(bank[sum_bank][32 * h:32 * h + 32, off:TT], v_aug[:, par, c, :],
                                         probs[:, s % (LAG + 1), h, off:TT], start=(c == 0),
                                         stop=(c == (TC // 2, TC)[half] - 1), skip_group_check=True)
                    last.then_inc(pv_done, 1)

                def products(it, par, s):
                    if s >= LAG:
                        product(it, par, s - LAG)
                    elif par == 1:
                        product(it, 0, s - LAG + NSTEP)
                    elif not isinstance(it, int) or it > 0:
                        product(it - 1, 1, s - LAG + NSTEP)

                def period(it, par, last=0, weights=True):
                    for s in range(NSTEP):
                        units = list(ahead(it, par, s, last))
                        if s == TURN and last == 1:
                            turn(it + par, 1 - par, followed=0)

                        def some(n):
                            for _ in range(min(n, len(units))):
                                at = units.pop(0)
                                if at[2] == NB:
                                    turn(it + par, 1 - par, followed=1)
                                unit(*at)

                        scores(it, par, s, 0)
                        some(1)
                        scores(it, par, s, 1)
                        some(1)
                        products(it, par, s)
                        some(2)

                pe.wait_ge(consts2, 3)
                pe.wait_ge(parts_set, 3)
                for u in range(NU):
                    unit(0, 0, u)
                for u in range(AHEAD):
                    if u == NB:
                        turn(0, 0, followed=1)
                    unit(0, 1, u)
                periods(pe, period)
                for s in range(NSTEP - LAG, NSTEP):
                    product(GROUPS // 2 - 1, 1, s)

            @block.vector
            def _(dve):
                def unit(it, par, u):
                    i, h0, nh, key, w, part = UNITS[u]
                    group = 2 * it + par
                    dve.wait_ge(unit_full, NU * group + u + 1)
                    bk = bank[unit_bank[u % NB]]
                    if key + w == (i + 1) * P:
                        settled(dve)
                        for k in range(nh):
                            cols = bk[:, k * w:(k + 1) * w]
                            last = dve.tensor_tensor_reduce(cols, cols, causal[:, TT - w:TT], 1.0, LEAST, ALU.add, ALU.max,
                                                            accum_out=max_parts[:, h0 + k, i, part:part + 1])
                    else:
                        last = dve.tensor_reduce(out=max_parts[:, h0:h0 + nh, i, part],
                                                 in_=bk[:, 0:nh * w].rearrange("p (k w) -> p k w", k=nh),
                                                 axis=AX.X, op=ALU.max)
                    last.then_inc(unit_free, 1)
                    if u == NU - 1:
                        dve.wait_ge(unit_free, NU * (group + 1))
                        wait_if(dve, negm_done, group)
                        chain = Chain(dve, d2, 2 * group)
                        chain.link(dve.tensor_reduce(out=neg_max_f[:], in_=max_parts[:].rearrange("p h i a -> p (h i) a"),
                                                     axis=AX.X, op=ALU.max, negate=True))
                        wait_if(dve, negt_full, group)
                        chain.link(dve.tensor_copy(neg_max[:, 0, :].bitcast(F32R), neg_max_f[:]))
                        dve.tensor_tensor(out=neg_max[:, 1, :].bitcast(F32R), in0=neg_max_f[:], in1=neg_max[:, 0, :],
                                          op=ALU.subtract).then_inc(negm_done, 1)

                def period(it, par, last=0, weights=True):
                    for s in range(NSTEP):
                        for at in ahead(it, par, s, last):
                            unit(*at)

                dve.memset(max_parts[:], LEAST).then_inc(parts_set, 1)
                for par in range(2):
                    dve.memset(kb[par][PROD:STACK, :].bitcast(F32), 1.0).then_inc(parts_set, 1)
                dve.wait_ge(parts_set, 3)
                for u in range(NU):
                    unit(0, 0, u)
                for u in range(AHEAD):
                    unit(0, 1, u)
                periods(dve, period)
                dve.wait_ge(l_in[0], 16)
                dve.reciprocal(l_sb[:], l_sb[:]).then_inc(l_recip, 1)
        core.close()
        attn.close()

        moe = ExitStack()
        h2_hi = sb(moe, "h2_hi", [P, DC, B * T], F32R)
        h2_lo = sb(moe, "h2_lo", [P, DC, B * T], F32R)
        cw = sb(moe, "cw", [P, NT, E], F32)

        post = ExitStack()
        l1_sb = sb(post, "l1_sb", [P, T // 4], F32)
        y_t = sb(post, "y_t", [P, NPASS, DC, TT], F32)
        r_t = sb(post, "r_t", [P, NPASS, DC, TT], F32)
        wo_gated = sb(post, "wo_gated", [P, B, DC, D], F32)
        xn2 = sb(post, "xn2", [P, 2, TJ, D], F32)
        h2 = sb(post, "h2", [P, 2, DC, TT], F32)

        y_in = [sem(f"y_loaded_{k}") for k in range(NPASS)]
        wo_done, yn_done, att_full = sem("wo_gated_done"), sem("yn_done"), sem("att_full")
        var2, sqrt2, xn2_done = sem("var2_ready"), sem("sqrt2_done"), sem("xn2_done")
        resid, xt2_full, h2_done, h2_hi_s, h2_lo_s = sem("residual_done"), sem("xt2_full"), sem("h2_done"), sem("h2_high_done"), sem("h2_low_done")
        lg_full, d3 = sem("logits_full"), sem("dve_chain3")
        lg_bank, T_BANKS = 6, (4, 0)

        def sums_in(eng, n):
            b, toks = n // 2, slice(n % 2 * TT, (n % 2 + 1) * TT)
            for m in range(DC):
                src = y_dram[b * NKV + 4 * m:b * NKV + 4 * m + 4, :, toks].rearrange("g (h r) t -> g h r t", r=32)
                eng.dma_start(y_t[:, n, m, :], src[:, :, 0:HD, :]).then_inc(y_in[n], 16)

        def recips_in(eng, n):
            b, toks = n // 2, slice(n % 2 * TT, (n % 2 + 1) * TT)
            for m in range(DC):
                src = r_dram[b, 16 * m:16 * m + 16, toks].unsqueeze(1).to_broadcast([16, HD, TT])
                eng.dma_start(r_t[:, n, m, :], src).then_inc(y_in[n], 16)

        with nc.Block() as block:
            @block.sync
            def _(sp):
                row_sums_in(sp, 1, l1_sb, l_in[1])
                sums_in(sp, 0)
                recips_in(sp, 0)
                sp.wait_ge(l_recip, 2)
                reciprocals_out(sp, 1, l1_sb)
                sums_in(sp, 1)
                recips_in(sp, 1)
                sums_in(sp, 2)
                sp.wait_ge(r_out[1], 16)
                recips_in(sp, 2)
                sums_in(sp, 3)
                recips_in(sp, 3)

            @block.gpsimd
            def _(pool):
                pool.wait_ge(yn_done, 1)
                for n in range(1, NPASS):
                    pool.wait_ge(y_in[n], 64)
                    pool.tensor_tensor(out=y_t[:, n], in0=y_t[:, n], in1=r_t[:, n], op=ALU.mult).then_inc(yn_done, 1)
                with pool.Fori(0, B) as b:
                    for half in range(2):
                        toks = bass.ds(b * T + half * TT, TT)
                        pool.wait_ge(h2_hi_s, DC * (2 * b + half + 1))
                        pool.tensor_tensor(out=h2_lo[:, :, toks], in0=h2[:, half], in1=h2_hi[:, :, toks].bitcast(F32),
                                           op=ALU.subtract).then_inc(h2_lo_s, 1)

            @block.scalar
            def _(act):
                for b in range(B):
                    square_roots(act, b, var2, sqrt2)
                    for half in range(2):
                        n = 2 * b + half + 1
                        for c in range(DC):
                            act.wait_ge(xt2_full, DC * (n - 1) + c + 1)
                            if n > 2 and c == 0:
                                act.wait_ge(h2_lo_s, n - 2)
                                act.wait_ge(lg_full, n - 2)
                            for to, done in ((h2[:, half, c, :], h2_done), (h2_hi[:, c, (n - 1) * TT:n * TT], h2_hi_s)):
                                act.activation(to, bank[T_BANKS[half] + c][:], ACT.Identity, scale=modc[:, b, 1, c, 0:1],
                                               bias=modc[:, b, 1, c, 1:2]).then_inc(done, 1)

            @block.tensor
            def _(pe):
                def output(n):
                    pe.wait_ge(yn_done, n)
                    if n > 2:
                        pe.wait_ge(resid, n - 2)
                    for j in range(TJ):
                        for m in range(DC):
                            last = pe.matmul(bank[2 * ((n - 1) % 2) + j // 2][:, (j % 2) * D:(j % 2 + 1) * D],
                                             y_t[:, n - 1, m, j * P:(j + 1) * P],
                                             wo_gated[:, (n - 1) // 2, m, :], start=(m == 0), stop=(m == DC - 1))
                    last.then_inc(att_full, 1)

                def transposes(n):
                    half = (n - 1) % 2
                    pe.wait_ge(xn2_done, n)
                    if n > 2:
                        pe.wait_ge(h2_hi_s, DC * (n - 2))
                    elif n == 2:
                        pe.wait_ge(resid, 3)
                    for c in range(DC):
                        for j in range(TJ):
                            last = pe.transpose(bank[T_BANKS[half] + c][:, j * P:(j + 1) * P],
                                                xn2[:, half, j, c * P:(c + 1) * P], ident[:])
                        last.then_inc(xt2_full, 1)

                def router(n):
                    half = (n - 1) % 2
                    pe.wait_ge(h2_done, DC * n)
                    for j in range(TJ):
                        tile = (n - 1) * TJ + j
                        for c in range(DC):
                            last = pe.matmul(bank[lg_bank][:, tile * E:(tile + 1) * E],
                                             h2[:, half, c, j * P:(j + 1) * P], wr_sb[:, c, :],
                                             start=(c == 0), stop=(c == DC - 1))
                    last.then_inc(lg_full, 1)

                pe.wait_ge(wo_done, B)
                for n in range(1, NPASS + 1):
                    output(n)
                transposes(1)
                transposes(2)
                for n in range(1, NPASS + 1):
                    router(n)
                    if n + 2 <= NPASS:
                        transposes(n + 2)

            @block.vector
            def _(dve):
                chain = Chain(dve, d3, 0)
                link = chain.link

                def residual(n):
                    half, tiles = (n - 1) % 2, slice((n - 1) * TJ, n * TJ)
                    dve.wait_ge(att_full, n)
                    dve.tensor_tensor(out=x_sb[:, tiles, :], in0=x_sb[:, tiles, :],
                                      in1=psum[:, 2 * half:2 * half + 2, :].rearrange("p a (c d) -> p (a c) d", c=2),
                                      op=ALU.add).then_inc(resid, 1)
                    dve.wait_ge(resid, n)
                    moments(dve, link, (n - 1) * TJ)

                def normal(n):
                    normalise(dve, (n - 1) * TJ, xn2[:, (n - 1) % 2]).then_inc(xn2_done, 1)

                for b in range(B):
                    dve.tensor_tensor(out=wo_gated[:, b], in0=wo_sb[:], in1=gate[:, 0, b:b + 1, :].to_broadcast([P, DC, D]),
                                      op=ALU.mult).then_inc(wo_done, 1)
                dve.wait_ge(l_in[1], 16)
                dve.reciprocal(l1_sb[:], l1_sb[:]).then_inc(l_recip, 1)
                dve.wait_ge(y_in[0], 64)
                dve.tensor_tensor(out=y_t[:, 0], in0=y_t[:, 0], in1=r_t[:, 0], op=ALU.mult).then_inc(yn_done, 1)
                residual(1)
                residual(2)
                deviations(dve, link, 0, var2, sqrt2)
                normal(1)
                normal(2)
                residual(3)
                residual(4)
                deviations(dve, link, 1, var2, sqrt2)
                for n in (3, 4):
                    dve.wait_ge(xt2_full, DC * (n - 2))
                    normal(n)
        post.close()

        wl_hi = sb(moe, "wl_hi", [P, NLATE, WCOLS], F32R)
        wl_lo = sb(moe, "wl_lo", [P, NLATE, WCOLS], F32R)
        wl_raw = sb(moe, "wl_raw", [P, 2, WCOLS], F32)
        mid = sb(moe, "mid", [P, 2, TT], F32)
        g_hi = sb(moe, "g_hi", [P, 2, TT], F32R)
        g_lo = sb(moe, "g_lo", [P, 2, TT], F32R)
        iota16 = sb(moe, "iota16", [P, E], F32)
        lg = sb(moe, "lg", [P, NT, E], F32)
        lmax = sb(moe, "lmax", [P, NT], F32)
        top = sb(moe, "top", [P, NT, 8], F32)
        top_i = sb(moe, "top_i", [P, NT, 8], U32)
        top_f = sb(moe, "top_f", [P, NT, 8], F32)
        wsum = sb(moe, "wsum", [P, NT], F32)
        acc = sb(moe, "acc", [P, TJ, D], F32)
        fin = sb(moe, "fin", [P, TJ, D], F32)
        hit = fin[:].rearrange("p a d -> p (a d)").rearrange("p (j r e) -> p j r e", j=NT, r=TOPK)
        wl_in, wl_hi_s, wl_lo_s = [sem(f"late_w_loaded_{k}") for k in range(2)], sem("late_w_high"), sem("late_w_low")
        up_full, silu_done, mult_done = sem("up_full"), sem("silu_done"), sem("mult_done")
        ghi_done, glo_done, down_done, acc_done = sem("g_high_done"), sem("g_low_done"), sem("down_done"), sem("acc_done")
        lg_ready, lg_exp, iota_s, d4 = sem("logits_ready"), sem("logits_exp"), sem("iota_ready"), sem("dve_chain4")
        ffn_done, o_out = sem("ffn_done"), sem("out_written")
        gated, fin_done = [[sem(f"{n}_{who}") for who in ("pool", "dve")] for n in ("ffn_gated", "out_ready")]
        POOLJ = 1
        NACC = E + 1

        def weights(e):
            return (w_hi[:, e, :], w_lo[:, e, :]) if e < NEARLY else (wl_hi[:, e - NEARLY, :], wl_lo[:, e - NEARLY, :])

        with nc.Block() as block:
            @block.sync
            def _(sp):
                for k in range(NLATE):
                    e = NEARLY + k
                    if k >= 2:
                        sp.wait_ge(wl_lo_s, k - 1)
                    if e < E:
                        load_expert(sp, wl_raw[:, k % 2, :], we1_in[e], we3_in[e], we2_in[e], wl_in[k % 2])
                    else:
                        cols = slice((e - E) * H, (e - E + 1) * H)
                        load_expert(sp, wl_raw[:, k % 2, :], ws1_in[:, cols], ws3_in[:, cols], ws2_in[cols, :], wl_in[k % 2])
                for t in range(NPASS):
                    sp.wait_ge(fin_done[0], t + 2)
                    sp.wait_ge(fin_done[1], t + 1)
                    sp.dma_start(out_view[:, t * TJ:(t + 1) * TJ, :], x_sb[:, t * TJ:(t + 1) * TJ, :]).then_inc(o_out, 16)
                sp.wait_ge(o_out, 16 * (B * T // TT))

            @block.gpsimd
            def _(pool):
                pool.iota(iota16[:], pattern=[[1, E]], base=0, channel_multiplier=0,
                          allow_small_or_imprecise_dtypes=True).then_inc(iota_s, 1)
                for k in range(NLATE):
                    pool.wait_ge(wl_in[k % 2], 48 * (k // 2 + 1))
                    pool.tensor_copy(wl_hi[:, k, :], wl_raw[:, k % 2, :]).then_inc(wl_hi_s, 1)
                    pool.wait_ge(wl_hi_s, k + 1)
                    pool.tensor_tensor(out=wl_lo[:, k, :], in0=wl_raw[:, k % 2, :], in1=wl_hi[:, k, :].bitcast(F32),
                                       op=ALU.subtract).then_inc(wl_lo_s, 1)
                with pool.Fori(0, B) as b, pool.Fori(0, 2) as half:
                    t = 2 * b + half
                    tiles = bass.ds(t * TJ, POOLJ)
                    pool.wait_ge(ffn_done, t + 1)
                    pool.tensor_tensor(out=fin[:, 0:POOLJ], in0=fin[:, 0:POOLJ],
                                       in1=gate[:, 1, bass.ds(b, 1), :].to_broadcast([P, POOLJ, D]), op=ALU.mult).then_inc(gated[0], 1)
                    pool.wait_ge(gated[0], t + 1)
                    pool.tensor_tensor(out=x_sb[:, tiles, :], in0=x_sb[:, tiles, :], in1=fin[:, 0:POOLJ], op=ALU.add)\
                        .then_inc(fin_done[0], 1)

            @block.scalar
            def _(act):
                act.wait_ge(lg_ready, 1)
                act.activation(lg[:], lg[:], ACT.Exp).then_inc(lg_exp, 1)
                with act.Fori(0, NPASS) as t:
                    def high(e):
                        act.wait_ge(mult_done, NE * t + e + 1 + 2)
                        act.wait_ge(down_done, NE * t + e - 1 + 2)
                        act.activation(g_hi[:, e % 2, :], mid[:, e % 2, :], ACT.Copy).then_inc(ghi_done, 1)
                    for e in range(NE):
                        act.wait_ge(up_full, NE * t + e + 1)
                        act.wait_ge(glo_done, NE * t + e - 1 + 2)
                        act.activation(mid[:, e % 2, :], bank[e % 2][:], ACT.Silu).then_inc(silu_done, 1)
                        if e:
                            high(e - 1)
                    high(NE - 1)

            @block.tensor
            def _(pe):
                pe.sem_inc(down_done, 2)
                with pe.Fori(0, NPASS) as t:
                    at = t * TT

                    def up(e):
                        hi, lo = weights(e)
                        if e >= NEARLY:
                            pe.wait_ge(wl_lo_s, e - NEARLY + 1)
                        pe.wait_ge(silu_done, NE * t + e - 1 + 2)
                        pe.wait_ge(mult_done, NE * t + e - 1 + 2)
                        for m in range(2):
                            n = 0
                            for w, h in ((hi, h2_hi), (lo, h2_hi), (hi, h2_lo)):
                                for c in range(DC):
                                    col = c * 2 * H + m * H
                                    last = pe.matmul(bank[2 * m + e % 2][:], w[:, col:col + H], h[:, c, bass.ds(at, TT)],
                                                     start=(n == 0), stop=(n == 5))
                                    n += 1
                        last.then_inc(up_full, 1)

                    def down(e):
                        hi, lo = weights(e)
                        pair = 4 + 2 * (min(e, E) % 2)
                        pe.wait_ge(glo_done, NE * t + e + 1 + 2)
                        if e <= E:
                            pe.wait_ge(acc_done, NACC * t + e - 1 + 2)
                        for g, w in ((g_hi, hi), (g_lo, hi), (g_hi, lo)):
                            for j in range(TJ):
                                first = e <= E and g is g_hi and w is hi and j % 2 == 0
                                last = pe.matmul(bank[pair + j // 2][:, (j % 2) * D:(j % 2 + 1) * D],
                                                 g[:, e % 2, j * P:(j + 1) * P], w[:, W13:WCOLS], start=first,
                                                 stop=((e < E or e == NE - 1) and w is lo), skip_group_check=True)
                        last.then_inc(down_done, 1)

                    for e in range(NE):
                        up(e)
                        if e >= 2:
                            down(e - 2)
                    down(NE - 2)
                    down(NE - 1)

            @block.vector
            def _(dve):
                for s_ in (glo_done, silu_done, mult_done, acc_done):
                    dve.sem_inc(s_, 2)
                dve.sem_inc(fin_done[0], 1)
                chain = Chain(dve, d4, 0)
                link = chain.link
                logits = bank[lg_bank][:, 0:NT * E].rearrange("p (j e) -> p j e", j=NT)
                link(dve.tensor_reduce(out=lmax[:], in_=logits, axis=AX.X, op=ALU.max))
                dve.tensor_tensor(out=lg[:], in0=logits, in1=lmax[:].unsqueeze(2).to_broadcast([P, NT, E]),
                                  op=ALU.subtract).then_inc(lg_ready, 1)
                dve.wait_ge(lg_exp, 1)
                settled(dve)
                for j in range(NT):
                    ins = dve.max(top[:, j, :], lg[:, j, :])
                link(ins)
                settled(dve)
                for j in range(NT):
                    ins = dve.max_index(top_i[:, j, :], top[:, j, :], lg[:, j, :])
                link(ins)
                dve.wait_ge(iota_s, 1)
                link(dve.tensor_copy(top_f[:], top_i[:]))
                for r in range(TOPK):
                    ins = dve.tensor_tensor(out=hit[:, :, r, :], in0=iota16[:].unsqueeze(1).to_broadcast([P, NT, E]),
                                            in1=top_f[:, :, r:r + 1].to_broadcast([P, NT, E]), op=ALU.is_equal)
                link(ins)
                link(dve.tensor_reduce(out=cw[:], in_=hit[:].rearrange("p j r e -> p j e r"), axis=AX.X, op=ALU.add))
                link(dve.tensor_tensor(out=cw[:], in0=cw[:], in1=lg[:], op=ALU.mult))
                link(dve.tensor_reduce(out=wsum[:], in_=cw[:], axis=AX.X, op=ALU.add))
                link(dve.reciprocal(wsum[:], wsum[:]))
                link(dve.tensor_scalar(wsum[:], wsum[:], float(TOPK), None, ALU.mult))
                link(dve.tensor_tensor(out=cw[:], in0=cw[:], in1=wsum[:].unsqueeze(2).to_broadcast([P, NT, E]), op=ALU.mult))
                with dve.Fori(0, B) as b, dve.Fori(0, 2) as half:
                    t = 2 * b + half

                    def low(e):
                        dve.wait_ge(ghi_done, NE * t + e + 1)
                        dve.tensor_tensor(out=g_lo[:, e % 2, :], in0=mid[:, e % 2, :], in1=g_hi[:, e % 2, :].bitcast(F32),
                                          op=ALU.subtract).then_inc(glo_done, 1)

                    def accumulate(e):
                        dve.wait_ge(down_done, NE * t + e + 1 + 2)
                        if e:
                            dve.wait_ge(acc_done, NACC * t + e + 2)
                        for j in range(TJ):
                            y = bank[4 + 2 * (e % 2) + j // 2][:, (j % 2) * D:(j % 2 + 1) * D]
                            weight = cw[:, t * TJ + j, e:e + 1]
                            if e:
                                last = dve.scalar_tensor_tensor(out=acc[:, j, :], in0=y, scalar=weight, in1=acc[:, j, :],
                                                                op0=ALU.mult, op1=ALU.add)
                            else:
                                last = dve.tensor_scalar(acc[:, j, :], y, weight, None, ALU.mult)
                        last.then_inc(acc_done, 1)

                    for e in range(NE):
                        m = mid[:, e % 2, :]
                        dve.wait_ge(silu_done, NE * t + e + 1 + 2)
                        dve.tensor_tensor(out=m, in0=m, in1=bank[2 + e % 2][:], op=ALU.mult).then_inc(mult_done, 1)
                        if e:
                            low(e - 1)
                        if 3 <= e < E + 3:
                            accumulate(e - 3)
                    low(NE - 1)
                    dve.wait_ge(down_done, NE * (t + 1) + 2)
                    dve.wait_ge(acc_done, NACC * t + E + 2)
                    dve.wait_ge(fin_done[0], t + 1)
                    dve.tensor_tensor(out=fin[:], in0=acc[:], in1=psum[:, 4:6, :].rearrange("p a (c d) -> p (a c) d", c=2),
                                      op=ALU.add).then_inc(ffn_done, 1)
                    dve.wait_ge(ffn_done, t + 1)
                    dve.sem_inc(acc_done, 1)
                    tiles = bass.ds(t * TJ + POOLJ, TJ - POOLJ)
                    dve.tensor_tensor(out=fin[:, POOLJ:TJ], in0=fin[:, POOLJ:TJ],
                                      in1=gate[:, 1, bass.ds(b, 1), :].to_broadcast([P, TJ - POOLJ, D]), op=ALU.mult).then_inc(gated[1], 1)
                    dve.wait_ge(gated[1], t + 1)
                    dve.tensor_tensor(out=x_sb[:, tiles, :], in0=x_sb[:, tiles, :], in1=fin[:, POOLJ:TJ], op=ALU.add)\
                       .then_inc(fin_done[1], 1)
        moe.close()


_INS = ["L0_attn_x", "L0_attn_wq", "L0_attn_wk", "L0_attn_wv", "L0_attn_wo", "L0_ffn_w_router", "L0_ffn_we1",
        "L0_ffn_we3", "L0_ffn_we2", "L0_ffn_ws1", "L0_ffn_ws3", "L0_ffn_ws2", "L0_c", "L0_wmod"]


def kernel(**inputs):
    import numpy as _np
    import concourse.bacc as _bacc
    from concourse import mybir as _mybir
    from concourse.bass_utils import run_bass_kernel_spmd as _run

    nc = _bacc.Bacc("TRN2", target_bir_lowering=False, num_devices=1)
    arrays, args = {}, []
    for name in _INS:
        a = _np.asarray(inputs[name])
        if name == "L0_attn_wq":
            a = a.reshape(D, NKV, REP, HD).transpose(0, 1, 3, 2).reshape(D, NH * HD)
        a = _np.ascontiguousarray(a)
        arrays[f"in_{name}_dram"] = a
        args.append(nc.dram_tensor(f"in_{name}_dram", a.shape, _mybir.dt.from_np(a.dtype), kind="ExternalInput").ap())
    args.append(nc.dram_tensor("out_0_dram", (B, T, D), _mybir.dt.float32, kind="ExternalOutput").ap())
    block_kernel(nc, *args)
    r = _run(nc, [arrays], core_ids=[0])
    return r.results[0]["out_0_dram"]
```
